# Optimizing a Trainium2 kernel written in Bass

```python
import numpy as np
import jax
import jax.numpy as jnp

def _softmax(x, axis=-1):
    return jax.nn.softmax(x, axis=axis)

def _gelu(x):
    return jax.nn.gelu(x, approximate=True)

def _silu(x):
    return jax.nn.silu(x)

def _sigmoid(x):
    return jax.nn.sigmoid(x)

def _layernorm(x, axis=-1, eps=1e-05):
    m = jnp.mean(x, axis=axis, keepdims=True)
    v = jnp.var(x, axis=axis, keepdims=True)
    return (x - m) / jnp.sqrt(v + eps)

def _scatter_add(tgt, idx, src, axis=0):
    return tgt.at[idx].add(src)

def _segment_sum(src, seg, n):
    return jax.ops.segment_sum(src, seg, n)
kernel_name = 'mk_xattn_ffn_d1_seqx_r8_9e84fe'

def setup_inputs(seed: int=0):
    np.random.seed(seed)
    _w = jnp.asarray

    def _rec_inputs():
        import jax
        import jax.numpy as jnp
        _rk = jax.random.key(seed)
        x = -0.0003929 + 0.9999 * jax.random.normal(jax.random.fold_in(_rk, 1), (4, 256, 256), jnp.float32)
        _lenS = 256 - jax.random.randint(jax.random.fold_in(_rk, 7), (4,), 0, max(1, 256 // 4) + 1, jnp.int32)
        _lenS2 = 256 - jax.random.randint(jax.random.fold_in(_rk, 8), (4,), 0, max(1, 256 // 4) + 1, jnp.int32)
        _ctx_1024P = jax.random.normal(jax.random.fold_in(_rk, 11), (4, 16, 128), jnp.float32)
        _ctx_1024c = jax.random.dirichlet(jax.random.fold_in(_rk, 511), 0.3 * jnp.ones((16,), jnp.float32), (4, 256))
        _ctx_1024t = jnp.einsum('bsk,bkd->bsd', _ctx_1024c, _ctx_1024P)
        _ctx_1024t = _ctx_1024t * jax.lax.rsqrt(jnp.mean(jnp.square(_ctx_1024t)) + 1e-12) * 0.953939
        ctx_1024 = 0.000227908 + 0.99994 * (_ctx_1024t + 0.3 * jax.random.normal(jax.random.fold_in(_rk, 611), (4, 256, 128), jnp.float32))
        return (x, ctx_1024)
    x, ctx_1024 = _rec_inputs()

    def _L0_xattn_setup():
        import jax, jax.numpy as jnp
        import numpy as np
        EPS = 1e-05

        def rmsnorm(x, g, eps=EPS):
            var = jnp.mean(jnp.square(x), axis=-1, keepdims=True)
            return x * jax.lax.rsqrt(var + eps) * g
        key = jax.random.key(seed)
        ks = jax.random.split(key, 8)
        B, Sq, Skv = (2, 512, 64)
        dim, cdim, H, D = (256, 128, 16, 128)
        inner = H * D
        s = lambda f: 1.0 / np.sqrt(f)
        return {'hidden_states': jax.random.normal(ks[0], (B, Sq, dim), jnp.float32), 'encoder_hidden_states': jax.random.normal(ks[1], (B, Skv, cdim), jnp.float32), 'Wq': jax.random.normal(ks[2], (dim, inner), jnp.float32) * s(dim), 'Wk': jax.random.normal(ks[3], (cdim, inner), jnp.float32) * s(cdim), 'Wv': jax.random.normal(ks[4], (cdim, inner), jnp.float32) * s(cdim), 'Wo': jax.random.normal(ks[5], (inner, dim), jnp.float32) * s(inner), 'gq': jnp.ones((D,), jnp.float32), 'gk': jnp.ones((D,), jnp.float32)}
    _L0_xattn_all = _L0_xattn_setup()
    _L0_xattn_in = {k: v for k, v in _L0_xattn_all.items() if k in ('Wq', 'Wk', 'Wv', 'Wo', 'gq', 'gk')}
    del _L0_xattn_all

    def _L0_ffn_setup():
        import jax, jax.numpy as jnp
        import numpy as np
        DIM = 256
        HIDDEN = 1024
        GROUP = 64

        def _ternary_weight(w, group_size):
            wb = w.astype(jnp.bfloat16)
            wg = wb.reshape(-1, group_size)
            scale = jnp.clip(jnp.mean(jnp.abs(wg), axis=-1, keepdims=True), 1e-08, None)
            q = jnp.clip(jnp.round(wg / scale), -1.0, 1.0)
            qs = (q * scale).reshape(w.shape).astype(w.dtype)
            return w + jax.lax.stop_gradient(qs - w)

        def _rms_norm(x):
            eps = jnp.asarray(jnp.finfo(x.dtype).eps, x.dtype)
            ms = jnp.mean(jnp.square(x), axis=-1, keepdims=True)
            return x * jax.lax.rsqrt(ms + eps)
        key = jax.random.key(seed)
        k_x, k_fc, k_proj = jax.random.split(key, 3)
        x = jax.random.normal(k_x, (4, 512, DIM), dtype=jnp.float32)
        W_fc = jax.random.normal(k_fc, (HIDDEN, DIM), dtype=jnp.float32) / np.sqrt(DIM)
        W_proj = jax.random.normal(k_proj, (DIM, HIDDEN), dtype=jnp.float32) / np.sqrt(HIDDEN)
        return {'x': x, 'W_fc': W_fc, 'W_proj': W_proj}
    _L0_ffn_all = _L0_ffn_setup()
    _L0_ffn_in = {k: v for k, v in _L0_ffn_all.items() if k in ('W_fc', 'W_proj')}
    del _L0_ffn_all
    return {'x': x, 'ctx_1024': ctx_1024, 'L0_xattn_Wq': _L0_xattn_in['Wq'], 'L0_xattn_Wk': _L0_xattn_in['Wk'], 'L0_xattn_Wv': _L0_xattn_in['Wv'], 'L0_xattn_Wo': _L0_xattn_in['Wo'], 'L0_xattn_gq': _L0_xattn_in['gq'], 'L0_xattn_gk': _L0_xattn_in['gk'], 'L0_ffn_W_fc': _L0_ffn_in['W_fc'], 'L0_ffn_W_proj': _L0_ffn_in['W_proj']}

def reference(x, ctx_1024, L0_xattn_Wq, L0_xattn_Wk, L0_xattn_Wv, L0_xattn_Wo, L0_xattn_gq, L0_xattn_gk, L0_ffn_W_fc, L0_ffn_W_proj):
    import jax
    import jax.numpy as jnp

    def _L0_xattn_ref(hidden_states, encoder_hidden_states, Wq, Wk, Wv, Wo, gq, gk):
        import jax, jax.numpy as jnp
        import numpy as np
        EPS = 1e-05

        def rmsnorm(x, g, eps=EPS):
            var = jnp.mean(jnp.square(x), axis=-1, keepdims=True)
            return x * jax.lax.rsqrt(var + eps) * g
        B, Sq, _ = hidden_states.shape
        Skv = encoder_hidden_states.shape[1]
        D = gq.shape[0]
        H = Wq.shape[1] // D
        scale = 1.0 / np.sqrt(D)
        q = (hidden_states @ Wq).reshape(B, Sq, H, D)
        k = (encoder_hidden_states @ Wk).reshape(B, Skv, H, D)
        v = (encoder_hidden_states @ Wv).reshape(B, Skv, H, D)
        q = rmsnorm(q, gq)
        k = rmsnorm(k, gk)
        scores = jnp.einsum('bqhd,bkhd->bhqk', q, k) * scale
        attn = jax.nn.softmax(scores, axis=-1)
        out = jnp.einsum('bhqk,bkhd->bqhd', attn, v)
        out = out.reshape(B, Sq, H * D)
        return out @ Wo

    def _L0_ffn_ref(x, W_fc, W_proj):
        import jax, jax.numpy as jnp
        import numpy as np
        DIM = 256
        HIDDEN = 1024
        GROUP = 64

        def _ternary_weight(w, group_size):
            wb = w.astype(jnp.bfloat16)
            wg = wb.reshape(-1, group_size)
            scale = jnp.clip(jnp.mean(jnp.abs(wg), axis=-1, keepdims=True), 1e-08, None)
            q = jnp.clip(jnp.round(wg / scale), -1.0, 1.0)
            qs = (q * scale).reshape(w.shape).astype(w.dtype)
            return w + jax.lax.stop_gradient(qs - w)

        def _rms_norm(x):
            eps = jnp.asarray(jnp.finfo(x.dtype).eps, x.dtype)
            ms = jnp.mean(jnp.square(x), axis=-1, keepdims=True)
            return x * jax.lax.rsqrt(ms + eps)
        w1 = _ternary_weight(W_fc, GROUP)
        h = jnp.einsum('bsd,hd->bsh', x, w1)
        h = jnp.square(jax.nn.relu(h))
        hn = _rms_norm(h)
        w2 = _ternary_weight(W_proj, GROUP)
        return jnp.einsum('bsh,dh->bsd', hn, w2)
    x = x + _L0_xattn_ref(_layernorm(x, axis=-1), ctx_1024, L0_xattn_Wq, L0_xattn_Wk, L0_xattn_Wv, L0_xattn_Wo, L0_xattn_gq, L0_xattn_gk)
    x = x + _L0_ffn_ref(_layernorm(x, axis=-1), L0_ffn_W_fc, L0_ffn_W_proj)
    return x

_drawn_inputs = setup_inputs


def setup_inputs(seed=0):
    import zlib

    import numpy as np

    out = dict(_drawn_inputs(seed))
    spreads = {'L0_xattn_gq': (1.0, 0.2), 'L0_xattn_gk': (1.0, 0.2)}
    factors = {}
    for name, (base, spread) in spreads.items():
        noise = np.random.default_rng([zlib.crc32(name.encode()), seed]).standard_normal(out[name].shape)
        drawn = base * np.exp(spread * noise) if base else spread * noise
        out[name] = jnp.asarray(drawn.astype(out[name].dtype))
    for name, factor in factors.items():
        out[name] = (out[name] * factor).astype(out[name].dtype)
    return out
```

```python
import concourse.bass as bass
from concourse import mybir
from contextlib import ExitStack


def xattn_ffn(nc, x, ctx, Wq, Wk, Wv, Wo, gq, gk, W_fc, W_proj, out):
    f32 = mybir.dt.float32
    f32r = mybir.dt.float32r
    bf16 = mybir.dt.bfloat16
    ALU = mybir.AluOpType
    ACT = mybir.ActivationFunctionType
    AX = mybir.AxisListType

    P = 128
    B, SQ, DIM = x.shape
    SKV, CD = ctx.shape[1:]
    D = gq.shape[0]
    H = Wq.shape[1] // D
    HID = W_fc.shape[0]
    GROUP = 64
    NT = B * SQ // P
    KC = DIM // P
    HT = HID // P
    HALF = B * SQ // 2
    QT = SQ // P
    KT = SKV // P
    T4 = HALF // P
    PAIRS = H // 2
    STEPS = B * PAIRS
    UT = 2 * KT
    NG = 2 * KC * HID // GROUP
    SG = NG // STEPS
    EPS = 1e-5
    EPS_F = 2.0 ** -23
    CLIP = 1.00117176771164e-08

    x_v = x.rearrange("b (t p) d -> p (b t) d", p=P)
    ctx_v = ctx.rearrange("b (t p) d -> p (b t) d", p=P)
    out_v = out.rearrange("b (t p) d -> p (b t) d", p=P)
    flat3 = "p a b -> p (a b)"

    es = ExitStack()
    with es:
        def sb(name, shape, dt=f32):
            return es.enter_context(nc.sbuf_tensor(name, shape, dt))

        def sem(name):
            return es.enter_context(nc.semaphore(name))

        xt = sb("xt", [P, NT, DIM])
        ct = sb("ct", [P, NT, CD])
        Wqr = sb("Wqr", [P, KC, 2, D])
        Wkr = sb("Wkr", [P, 2, D])
        Wvr = sb("Wvr", [P, H, D])
        Wor = sb("Wor", [P, H, DIM])
        gqt = sb("gqt", [P, 1])
        gkt = sb("gkt", [P, 1])
        gg = sb("gg", [P, 1])
        fpr = sb("fpr", [P, NG, GROUP])
        ident = sb("ident", [P, P])
        identb = sb("identb", [P, P], bf16)
        ones = sb("ones", [P, 1])
        mhalf = sb("mhalf", [P, UT])
        stats = sb("stats", [P, NT, 6])
        mv = sb("mv", [P, NT, 2])
        lnv = sb("lnv", [P, NT])
        rstd = sb("rstd", [P, NT])
        xn = sb("xn", [P, NT, DIM])
        xTh = sb("xTh", [P, B, KC, SQ], f32r)
        xTl = sb("xTl", [P, B, KC, SQ], f32r)
        cTh = sb("cTh", [P, NT, P], f32r)
        cTl = sb("cTl", [P, NT, P], f32r)
        ch = sb("ch", [P, NT, CD], f32r)
        cl = sb("cl", [P, NT, CD], f32r)
        WvT = xn[:, :, :].rearrange(flat3).rearrange("p (h c) -> p h c", h=H)
        WWh = sb("WWh", [P, H, DIM], f32r)
        WWl = sb("WWl", [P, H, DIM], f32r)
        wb = Wvr[:, :, :].rearrange(flat3).bitcast(bf16).rearrange("p (n k) -> p n k", k=GROUP)
        wabs = sb("wabs", [P, SG, GROUP], bf16)
        gsum = sb("gsum", [P, NG])
        gsr = sb("gsr", [P, SG], bf16)
        wpos = sb("wpos", [P, SG, GROUP], bf16)
        wneg = sb("wneg", [P, SG, GROUP], bf16)
        wt = Wor[:, 0:H // 2, :].rearrange(flat3).bitcast(bf16).rearrange("p (n k) -> p n k", k=GROUP)
        w1b = wt[:, 0:NG // 2, :].rearrange(flat3).rearrange("p (j d) -> p j d", j=HT)
        w2b = wt[:, NG // 2:NG, :].rearrange(flat3).rearrange("p (c h) -> p c h", c=KC)
        w1T = sb("w1T", [P, KC, HID], f32r)
        w2T = sb("w2T", [P, HT, DIM], f32r)
        Wqh = sb("Wqh", [P, KC, 2, D], f32r)
        Wql = sb("Wql", [P, KC, 2, D], f32r)
        Wkh = sb("Wkh", [P, 2, D], f32r)
        Wkl = sb("Wkl", [P, 2, D], f32r)
        ksq = sb("ksq", [P, UT, D])
        ssk = sb("ssk", [P, UT])
        kv = sb("kv", [P, UT])
        rk = sb("rk", [P, UT])
        kn = sb("kn", [P, UT, D])
        kh = sb("kh", [P, 2, SKV], f32r)
        kl = sb("kl", [P, 2, SKV], f32r)
        qsq = sb("qsq", [P, 2, SQ])
        qh = sb("qh", [P, 2, SQ], f32r)
        ql = sb("ql", [P, 2, SQ], f32r)
        qv = sb("qv", [P, UT])
        fq = sb("fq", [P, UT])
        mx = [sb(f"mx{u}", [P, QT]) for u in range(2)]
        nb = [sb(f"nb{u}", [P, QT]) for u in range(2)]
        su = [sb(f"su{u}", [P, QT]) for u in range(2)]
        rs = [sb(f"rs{u}", [P, QT]) for u in range(2)]
        Pr = [sb(f"Pr{u}", [P, QT, SKV]) for u in range(2)]
        PTh = [sb(f"PTh{u}", [P, KT, SQ], f32r) for u in range(2)]
        PTl = [sb(f"PTl{u}", [P, KT, SQ], f32r) for u in range(2)]
        Oh = [sb(f"Oh{u}", [P, SQ], f32r) for u in range(2)]
        Ol = [sb(f"Ol{u}", [P, SQ], f32r) for u in range(2)]
        hr = [Pr[0][:, :, :].rearrange(flat3), Pr[1][:, :, :].rearrange(flat3)]
        hs = [kn[:, :, :].rearrange(flat3), ksq[:, :, :].rearrange(flat3)]
        h4 = [qsq[:, :, :].rearrange(flat3), Wor[:, H // 2:H // 2 + 2, :].rearrange(flat3)]
        ha = ct[:, :, :].rearrange(flat3).rearrange("p (g t) -> p g t", g=2)
        fv = sb("fv", [P, NT])
        fr = sb("fr", [P, NT])
        yo = xn

        def bank(name):
            return es.enter_context(nc.psum_tensor(name, [P, 512], f32))

        bA = bank("bA")
        bB = bank("bB")
        bS = [bank("bS0"), bank("bS1")]
        bT = [bank("bT0"), bank("bT1")]
        bO = bank("bO")
        bY = bank("bY")

        s_x = [sem("s_x0"), sem("s_x1")]; s_c = sem("s_c"); s_g = sem("s_g"); s_wq = sem("s_wq"); s_wk = sem("s_wk")
        s_wv = sem("s_wv"); s_wo = [sem("s_wo0"), sem("s_wo1")]; s_fc = sem("s_fc"); s_pj = sem("s_pj")
        s_out = sem("s_out")
        s_own = sem("s_own"); s_const0 = sem("s_const0"); s_const = sem("s_const")
        s_mh = sem("s_mh"); s_gg = sem("s_gg")
        s_st = sem("s_st"); s_mv = sem("s_mv"); s_lnv = sem("s_lnv"); s_rstd = sem("s_rstd"); s_xn = sem("s_xn")
        s_turn = sem("s_turn")
        s_th = sem("s_th"); s_tl = sem("s_tl")
        s_ch = sem("s_ch"); s_cl = sem("s_cl")
        s_wvT = sem("s_wvT"); s_wvc = sem("s_wvc")
        s_ww = sem("s_ww"); s_wwh = sem("s_wwh"); s_wwl = sem("s_wwl")
        t_wb = sem("t_wb"); t_sum = sem("t_sum"); t_scr = sem("t_scr")
        t_pn = sem("t_pn"); t_dif = sem("t_dif"); t_done = sem("t_done")
        s_wt = sem("s_wt"); s_wtc = [sem("s_wtc0"), sem("s_wtc1")]
        wqh_done = sem("wqh_done"); wq_done = sem("wq_done"); wkh_done = sem("wkh_done"); wk_done = sem("wk_done")
        k_done = sem("k_done"); q_done = sem("q_done"); kt_done = sem("kt_done"); ssq_done = sem("ssq_done")
        s_done = [sem("s_done0"), sem("s_done1")]
        pt_done = [sem("pt_done0"), sem("pt_done1")]
        av_done = sem("av_done"); y_done = sem("y_done")
        ksq_done = sem("ksq_done"); qsq_done = sem("qsq_done"); qh_done = sem("qh_done")
        pth_done = [sem("pth_done0"), sem("pth_done1")]
        kh_done = sem("kh_done"); oh_done = sem("oh_done")
        exp_done = [sem("exp_done0"), sem("exp_done1")]
        red_done = sem("red_done"); kv_done = sem("kv_done"); kn_done = sem("kn_done"); ql_done = sem("ql_done")
        ptl_done = [sem("ptl_done0"), sem("ptl_done1")]
        kl_done = sem("kl_done"); ol_done = sem("ol_done"); qv_done = sem("qv_done")
        mx_done = [sem("mx_done0"), sem("mx_done1")]
        nb_done = [sem("nb_done0"), sem("nb_done1")]
        rec_done = [sem("rec_done0"), sem("rec_done1")]
        pn_done = [sem("pn_done0"), sem("pn_done1")]
        rk_done = sem("rk_done"); fq_done = sem("fq_done"); x1_done = sem("x1_done")
        f1_done = sem("f1_done"); hr_done = sem("hr_done"); hs_done = sem("hs_done")
        sh_done = sem("sh_done"); sl_done = sem("sl_done"); h4_done = sem("h4_done"); ha_done = sem("ha_done")
        f2_done = sem("f2_done"); fs_done = sem("fs_done"); fv_done = sem("fv_done"); fr_done = sem("fr_done")
        yo_done = sem("yo_done")

        WWsteps = H // 2
        TURNS_C = NT * CD // 512
        turn_banks = [bS[0], bS[1], bT[0], bT[1], bO, bY]
        wv_banks = [bS[0], bS[1], bT[0], bT[1]]
        ww_banks = [bT[0], bT[1], bO, bY]
        wt_banks = [bS[0], bS[1], bT[0], bT[1]]
        x2_banks = [bO, bY, bT[0], bT[1]]
        sTh = WWh[:, :, :].rearrange(flat3).rearrange("p (j t) -> p j t", j=HT)
        sTl = WWl[:, :, :].rearrange(flat3).rearrange("p (j t) -> p j t", j=HT)
        h_banks = [bA, bB, bS[0]]
        f_banks = [[bS[1], bO], [bY, bT[0]]]
        fs_bank = bT[1]

        def known(n):
            return isinstance(n, int)

        block = es.enter_context(nc.Block())

        @block.sync
        def _(sp):
            def load_k(n, pair):
                if not known(n) or n >= 1:
                    sp.wait_ge(wk_done, n)
                sp.dma_start(Wkr[:, :, :].rearrange(flat3), Wk[:, bass.ds(2 * D * pair, 2 * D)]).then_inc(s_wk, 16)

            def load_q(n, pair):
                if not known(n) or n >= 1:
                    sp.wait_ge(wq_done, n)
                sp.dma_start(Wqr[:, :, :, :].rearrange("p c u d -> p c (u d)"),
                             Wq.rearrange("(c p) n -> p c n", p=P)[:, :, bass.ds(2 * D * pair, 2 * D)]).then_inc(s_wq, 16)

            sp.dma_start(xt[:, 0:QT, :], x_v[:, 0:QT, :]).then_inc(s_x[0], 16)
            sp.dma_start(ct[:, :, :], ctx_v).then_inc(s_c, 16)
            load_k(0, 0)
            load_q(0, 0)
            sp.dma_start(xt[:, QT:NT, :], x_v[:, QT:NT, :]).then_inc(s_x[1], 16)
            sp.dma_start(Wvr[:, :, :], Wv.rearrange("p (h d) -> p h d", d=D)).then_inc(s_wv, 16)
            for m in range(2):
                hs_ = slice(m * H // 2, (m + 1) * H // 2)
                sp.dma_start(Wor[:, hs_, :], Wo.rearrange("(h p) n -> p h n", p=P)[:, hs_, :]).then_inc(s_wo[m], 16)
            load_k(1, 1)
            load_q(1, 1)
            sp.dma_start(fpr[:, 0:NG // 2, :].rearrange(flat3).rearrange("p (j d) -> p j d", j=HT),
                         W_fc.rearrange("(j p) d -> p j d", p=P)).then_inc(s_fc, 16)
            sp.dma_start(fpr[:, NG // 2:NG, :].rearrange(flat3).rearrange("p (t h) -> p t h", t=KC),
                         W_proj.rearrange("(t p) h -> p t h", p=P)).then_inc(s_pj, 16)
            for b in range(B):
                f = b * PAIRS
                with sp.Fori(f + (0 if b else 2), f + PAIRS) as n:
                    load_k(n, n - f)
                    load_q(n, n - f)
            for n in range(4):
                sp.wait_ge(yo_done, n + 1)
                sp.dma_start(out_v[:, 2 * n:2 * n + 2, :], yo[:, 2 * n:2 * n + 2, :]).then_inc(s_out, 16)
            sp.wait_ge(s_out, 64)

        @block.gpsimd
        def _(gp):
            gp.memset(mhalf[:, :], -0.5).then_inc(s_mh, 1)
            gp.memset(ones[:, :], 1.0).then_inc(s_const, 1)
            gp.memset(ident[:, :], 0.0).then_inc(s_const0, 1)
            gp.memset(identb[:, :], 0.0).then_inc(s_const0, 1)
            gp.wait_ge(s_const0, 2)
            for m in (ident, identb):
                gp.affine_select(out=m[:, :], in_=m[:, :], compare_op=ALU.not_equal, fill=1.0,
                                 base=0, pattern=[[-1, P]], channel_multiplier=1).then_inc(s_const, 1)
            gp.wait_ge(s_mh, 1)

            def split(n, src, loaded, hi, lo, used, hi_done, done):
                if not known(n) or n >= 1:
                    gp.wait_ge(used, n)
                gp.wait_ge(loaded, 16 * (n + 1))
                gp.sem_inc(s_own, 1)
                gp.tensor_scalar(hi, src, 1.0, 1.0, ALU.mult, ALU.mult).then_inc(hi_done, 1)
                gp.wait_ge(hi_done, n + 1)
                gp.sem_inc(s_own, 1)
                gp.tensor_tensor(lo, src, hi.bitcast(f32), ALU.subtract).then_inc(done, 1)

            def split_q(n):
                flat = "p c u d -> p (c u d)"
                split(n, Wqr[:, :, :, :].rearrange(flat), s_wq, Wqh[:, :, :, :].rearrange(flat),
                      Wql[:, :, :, :].rearrange(flat), q_done, wqh_done, wq_done)

            def split_k(n):
                split(n, Wkr[:, :, :].rearrange(flat3), s_wk, Wkh[:, :, :].rearrange(flat3),
                      Wkl[:, :, :].rearrange(flat3), k_done, wkh_done, wk_done)

            def rsqrt_k(n):
                gp.wait_ge(kv_done, n + 1)
                gp.tensor_tensor(rk[:, :], kv[:, :], mhalf[:, :], ALU.pow).then_inc(rk_done, 1)

            def rsqrt_q(n):
                gp.wait_ge(qv_done, n + 1)
                gp.tensor_tensor(fq[:, :], qv[:, :], mhalf[:, :], ALU.pow).then_inc(fq_done, 1)

            def rsqrt_ln(call, b):
                s = slice(b * QT, (b + 1) * QT)
                gp.wait_ge(s_lnv, call)
                gp.tensor_tensor(rstd[:, s], lnv[:, s], mhalf[:, 0:QT], ALU.pow).then_inc(s_rstd, 1)

            def norm_p(n):
                gp.wait_ge(rec_done[0], n + 1)
                gp.sem_inc(s_own, 1)
                for t in range(QT):
                    last = gp.tensor_scalar(Pr[0][:, t, :], Pr[0][:, t, :], rs[0][:, t:t + 1], 1.0,
                                            ALU.mult, ALU.mult)
                last.then_inc(pn_done[0], 1)

            def ternary(i):
                gp.wait_ge(t_pn, i + 1)
                gp.tensor_tensor(wpos[:, :, :], wpos[:, :, :], wneg[:, :, :], ALU.subtract).then_inc(t_dif, 1)
                gp.wait_ge(t_dif, i + 1)
                gp.sem_inc(s_own, 1)
                gp.tensor_tensor(wt[:, bass.ds(SG * i, SG), :], wpos[:, :, :],
                                 gsr[:, :].unsqueeze(2).broadcast_to([P, SG, GROUP]), ALU.mult).then_inc(t_done, 1)

            split_k(0)
            split_q(0)
            rsqrt_ln(1, 0)
            rsqrt_k(0)
            split_k(1)
            split_q(1)
            rsqrt_q(0)
            for b in range(1, B):
                rsqrt_ln(b + 1, b)
            rsqrt_k(1)
            norm_p(0)
            split_k(2)

            def body(i, ln=None):
                if not known(i) or i + 3 < STEPS:
                    split_k(i + 3)
                if not known(i) or i + 1 < STEPS:
                    rsqrt_q(i + 1)
                if not known(i) or i + 2 < STEPS:
                    split_q(i + 2)
                    rsqrt_k(i + 2)
                if not known(i) or i + 1 < STEPS:
                    norm_p(i + 1)
                ternary(i)
                if ln is not None:
                    rsqrt_ln(B + ln + 1, ln)

            for b in range(B):
                f = b * PAIRS
                body(f, ln=b - 1 if b else None)
                with gp.Fori(f + 1, f + PAIRS if b < B - 1 else STEPS - 3) as i:
                    body(i)
            for i in range(STEPS - 3, STEPS):
                body(i)

            rsqrt_ln(2 * B, B - 1)
            for g in range(2):
                for j in range(HT):
                    m = g * HT + j
                    gp.wait_ge(h4_done, m + 1)
                    if j == 0:
                        gp.tensor_copy(ha[:, g, :], h4[m % 2]).then_inc(ha_done, 1)
                    else:
                        gp.wait_ge(ha_done, m)
                        gp.tensor_tensor(ha[:, g, :], ha[:, g, :], h4[m % 2], ALU.add).then_inc(ha_done, 1)
                gp.wait_ge(fv_done, g + 1)
                gp.tensor_tensor(fr[:, g * T4:(g + 1) * T4], fv[:, g * T4:(g + 1) * T4], mhalf[:, 0:T4],
                                 ALU.pow).then_inc(fr_done, 1)

        @block.scalar
        def _(act):
            act.dma_start(gqt[:, :], gq.rearrange("(p o) -> p o", o=1)).then_inc(s_g, 16)
            act.dma_start(gkt[:, :], gk.rearrange("(p o) -> p o", o=1)).then_inc(s_g, 16)

            def turned(n):
                act.wait_ge(s_turn, n + 1)
                if n < TURNS_C:
                    dst = cTh[:, 4 * n:4 * n + 4, :]
                else:
                    dst = xTh[:, n - TURNS_C, :, :]
                act.activation(dst.rearrange(flat3), turn_banks[n][:, :], ACT.Copy).then_inc(s_th, 1)

            def k_square(n):
                act.wait_ge(k_done, n + 1)
                act.activation(ksq[:, :, :].rearrange(flat3), bB[:, :], ACT.Square).then_inc(ksq_done, 1)

            def q_parts(n):
                act.wait_ge(q_done, n + 1)
                act.activation(qsq[:, :, :].rearrange(flat3), bA[:, :], ACT.Square).then_inc(qsq_done, 1)
                act.activation(qh[:, :, :].rearrange(flat3), bA[:, :], ACT.Copy).then_inc(qh_done, 1)

            def pt_hi(i, u):
                act.wait_ge(pt_done[u], i + 1)
                act.activation(PTh[u][:, :, :].rearrange(flat3), bT[u][:, :], ACT.Copy).then_inc(pth_done[u], 1)

            def k_hi(n):
                act.wait_ge(kt_done, n + 1)
                act.activation(kh[:, :, :].rearrange(flat3), bT[1][:, :], ACT.Copy, scale=gg[:, 0:1]).then_inc(kh_done, 1)

            def o_hi(i, u):
                act.wait_ge(av_done, 2 * i + u + 1)
                act.activation(Oh[u][:, :], bO[:, u * SQ:(u + 1) * SQ], ACT.Copy).then_inc(oh_done, 1)

            def exps(n, u):
                act.wait_ge(nb_done[u], n + 1)
                for t in range(QT):
                    last = act.activation(Pr[u][:, t, :], bS[u][:, t * SKV:(t + 1) * SKV], ACT.Exp,
                                          bias=nb[u][:, t:t + 1], scale=fq[:, QT * u + t:QT * u + t + 1],
                                          accum_out=su[u][:, t:t + 1])
                last.then_inc(exp_done[u], 1)

            def norm_p(i):
                act.wait_ge(rec_done[1], i + 1)
                for t in range(QT):
                    last = act.activation(Pr[1][:, t, :], Pr[1][:, t, :], ACT.Copy, scale=rs[1][:, t:t + 1])
                last.then_inc(pn_done[1], 1)

            def ternary(i):
                act.activation(wb[:, bass.ds(SG * i, SG), :].rearrange(flat3),
                               fpr[:, bass.ds(SG * i, SG), :].rearrange(flat3), ACT.Copy, scale=2.0).then_inc(t_wb, 1)
                act.wait_ge(t_wb, i + 1)
                for k in range(SG):
                    last = act.activation(wabs[:, k, :], wb[:, bass.ds(SG * i + k, 1), :].rearrange(flat3), ACT.Abs,
                                          accum_out=gsum[:, bass.ds(SG * i + k, 1)])
                last.then_inc(t_sum, 1)

            for n in range(TURNS_C + 1):
                turned(n)
            k_square(0)
            q_parts(0)
            act.activation(ch[:, :, :], ct[:, :, :], ACT.Copy).then_inc(s_ch, 1)
            act.wait_ge(s_gg, 1)
            k_hi(0)
            for n in range(TURNS_C + 1, TURNS_C + B):
                turned(n)
            k_square(1)
            exps(0, 0)
            exps(0, 1)
            for n in range(H // 4):
                act.wait_ge(s_wvT, n + 1)
                act.activation(WvT[:, 4 * n:4 * n + 4, :].rearrange(flat3), wv_banks[n][:, :], ACT.Copy).then_inc(s_wvc, 1)
            for n in range(WWsteps):
                act.wait_ge(s_ww, n + 1)
                act.activation(WWh[:, 2 * n:2 * n + 2, :].rearrange(flat3), ww_banks[n % 4][:, :],
                               ACT.Copy).then_inc(s_wwh, 1)
            act.wait_ge(s_fc, 16)
            act.wait_ge(s_pj, 16)

            def body(i):
                ahead = not known(i) or i + 1 < STEPS
                if ahead:
                    q_parts(i + 1)
                    k_hi(i + 1)
                pt_hi(i, 0)
                if not known(i) or i + 2 < STEPS:
                    k_square(i + 2)
                norm_p(i)
                ternary(i)
                o_hi(i, 0)
                pt_hi(i, 1)
                if ahead:
                    exps(i + 1, 0)
                o_hi(i, 1)
                if ahead:
                    exps(i + 1, 1)

            with act.Fori(0, STEPS - 2) as i:
                body(i)
            body(STEPS - 2)
            body(STEPS - 1)

            def weights(n):
                act.wait_ge(s_wt, n + 1)
                act.activation((w1T[:, n, :] if n < 2 else w2T[:, 4 * (n - 2):4 * (n - 2) + 4, :].rearrange(flat3)),
                               wt_banks[n][:, :].bitcast(bf16), ACT.Copy).then_inc(s_wtc[0], 1)

            def turned_2(b):
                act.wait_ge(s_turn, TURNS_C + B + b + 1)
                act.activation(xTh[:, b, :, :].rearrange(flat3), x2_banks[b][:, :], ACT.Copy).then_inc(s_th, 1)

            weights(0)
            turned_2(0)
            turned_2(1)
            weights(2)
            for m in range(2 * HT):
                if m == 2:
                    turned_2(2)
                    turned_2(3)
                act.wait_ge(f1_done, m + 1)
                act.activation(hr[m % 2], h_banks[m % 3][:, :], ACT.Relu).then_inc(hr_done, 1)
                act.wait_ge(hr_done, m + 1)
                if m >= 2:
                    act.wait_ge(sl_done, m - 1)
                act.activation(hs[m % 2], hr[m % 2], ACT.Square).then_inc(hs_done, 1)
                act.wait_ge(hs_done, m + 1)
                if m >= 2:
                    act.wait_ge(ha_done, m - 1)
                act.activation(h4[m % 2], hs[m % 2], ACT.Square).then_inc(h4_done, 1)

        @block.tensor
        def _(pe):
            def three(dst, sth, stl, mvh, mvl, start, stop, **kw):
                pe.matmul(dst, sth, mvh, start=start, stop=False, **kw)
                pe.matmul(dst, sth, mvl, start=False, stop=False, **kw)
                return pe.matmul(dst, stl, mvh, start=False, stop=stop, **kw)

            def turn_x(dst, b):
                for c in range(KC):
                    for t in range(QT):
                        last = pe.transpose(dst[:, (QT * c + t) * P:(QT * c + t + 1) * P],
                                            xn[:, QT * b + t, c * P:(c + 1) * P], ident[:, :])
                last.then_inc(s_turn, 1)

            def keys(n, b):
                pe.wait_ge(wk_done, n + 1)
                if not known(n) or n >= 1:
                    pe.wait_ge(kn_done, n)
                for t in range(KT):
                    last = three(bB[:, t * 2 * D:(t + 1) * 2 * D], cTh[:, KT * b + t, :], cTl[:, KT * b + t, :],
                                 Wkh[:, :, :].rearrange(flat3), Wkl[:, :, :].rearrange(flat3), True, True)
                last.then_inc(k_done, 1)

            def queries(n, b):
                pe.wait_ge(wq_done, n + 1)
                if not known(n) or n >= 1:
                    pe.wait_ge(qv_done, n)
                for u in range(2):
                    for c in range(KC):
                        last = three(bA[:, u * SQ:(u + 1) * SQ], Wqh[:, c, u, :], Wql[:, c, u, :],
                                     xTh[:, b, c, :], xTl[:, b, c, :], c == 0, c == KC - 1)
                last.then_inc(q_done, 1)

            def turn_p(i, u):
                pe.wait_ge(pn_done[u], i + 1)
                if u == 1 and (not known(i) or i + 1 < STEPS):
                    pe.wait_ge(kl_done, i + 2)
                elif not known(i) or i >= 1:
                    pe.wait_ge(ptl_done[u], i)
                for t in range(QT):
                    for k in range(KT):
                        last = pe.transpose(bT[u][:, k * SQ + t * P:k * SQ + (t + 1) * P],
                                            Pr[u][:, t, k * P:(k + 1) * P], ident[:, :])
                last.then_inc(pt_done[u], 1)

            def turn_k(n):
                pe.wait_ge(kn_done, n + 1)
                if not known(n) or n >= 2:
                    pe.wait_ge(ptl_done[1], n - 1)
                for t in range(KT):
                    for u in range(2):
                        last = pe.transpose(bT[1][:, u * SKV + t * P:u * SKV + (t + 1) * P], kn[:, 2 * t + u, :], ident[:, :])
                last.then_inc(kt_done, 1)

            def project(i, u, pair, start=False):
                pe.wait_ge(ol_done, 2 * i + u + 1)
                for t in range(QT):
                    s = slice(t * P, (t + 1) * P)
                    last = three(bY[:, t * DIM:(t + 1) * DIM], Oh[u][:, s], Ol[u][:, s],
                                 WWh[:, bass.ds(2 * pair + u, 1), :].rearrange(flat3),
                                 WWl[:, bass.ds(2 * pair + u, 1), :].rearrange(flat3),
                                 start and t == 0, False, skip_group_check=True)
                last.then_inc(y_done, 1)

            def attend(i, u, b):
                pe.wait_ge(ptl_done[u], i + 1)
                for k in range(KT):
                    last = three(bO[:, u * SQ:(u + 1) * SQ], ch[:, KT * b + k, :], cl[:, KT * b + k, :],
                                 PTh[u][:, k, :], PTl[u][:, k, :], k == 0, k == KT - 1)
                last.then_inc(av_done, 1)

            def sums_q(n):
                pe.wait_ge(qsq_done, n + 1)
                pe.wait_ge(ql_done, n + 1)
                for j in range(UT):
                    u, t = divmod(j, QT)
                    last = pe.matmul(bA[:, j:j + 1], qsq[:, u, t * P:(t + 1) * P], ones[:, :], start=True, stop=True)
                last.then_inc(ssq_done, 1)

            def scores(n, u):
                pe.wait_ge(kl_done, n + 1)
                if not known(n) or n >= 1:
                    pe.wait_ge(exp_done[u], n)
                for t in range(QT):
                    s = slice(t * P, (t + 1) * P)
                    last = three(bS[u][:, t * SKV:(t + 1) * SKV], qh[:, u, s], ql[:, u, s], kh[:, u, :], kl[:, u, :],
                                 True, True)
                last.then_inc(s_done[u], 1)

            pe.wait_ge(s_const, 3)
            pe.wait_ge(s_c, 16)
            for n in range(TURNS_C):
                for t in range(4):
                    last = pe.transpose(turn_banks[n][:, t * P:(t + 1) * P], ct[:, 4 * n + t, :], ident[:, :])
                last.then_inc(s_turn, 1)
            pe.wait_ge(s_xn, 1)
            turn_x(turn_banks[TURNS_C], 0)
            pe.wait_ge(s_tl, TURNS_C)
            keys(0, 0)
            pe.wait_ge(s_tl, TURNS_C + 1)
            queries(0, 0)
            turn_k(0)
            sums_q(0)
            for b in range(1, B):
                pe.wait_ge(s_xn, b + 1)
                if b == 1:
                    pe.wait_ge(kl_done, 1)
                turn_x(turn_banks[TURNS_C + b], b)
            keys(1, 0)
            pe.wait_ge(s_tl, TURNS_C)
            scores(0, 0)
            scores(0, 1)
            pe.wait_ge(s_wv, 16)
            pe.wait_ge(s_tl, TURNS_C + B)
            for n in range(H // 4):
                if n < 2:
                    pe.wait_ge(exp_done[n], 1)
                for t in range(4):
                    last = pe.transpose(wv_banks[n][:, t * P:(t + 1) * P], Wvr[:, 4 * n + t, :], ident[:, :])
                last.then_inc(s_wvT, 1)
            for n in range(WWsteps):
                pe.wait_ge(s_wo[n // 4], 16)
                pe.wait_ge(s_wvc, 4)
                if n >= 4:
                    pe.wait_ge(s_wwl, n - 3)
                for t in range(2):
                    last = pe.matmul(ww_banks[n % 4][:, t * DIM:(t + 1) * DIM], WvT[:, 2 * n + t, :],
                                     Wor[:, 2 * n + t, :], start=True, stop=True)
                last.then_inc(s_ww, 1)
            pe.wait_ge(s_wwl, WWsteps)
            pe.wait_ge(s_cl, 1)

            def body(i, b, bn, bm, pair, before, start=False):
                ahead = not known(i) or i + 1 < STEPS
                if ahead:
                    queries(i + 1, bn)
                if before is not None:
                    project(i - 1, 1, before)
                if ahead:
                    turn_k(i + 1)
                turn_p(i, 0)
                if not known(i) or i + 2 < STEPS:
                    keys(i + 2, bm)
                if ahead:
                    sums_q(i + 1)
                    scores(i + 1, 0)
                attend(i, 0, b)
                turn_p(i, 1)
                if ahead:
                    scores(i + 1, 1)
                if start and b:
                    pe.wait_ge(x1_done, b)
                project(i, 0, pair, start)
                attend(i, 1, b)

            for b in range(B):
                f = b * PAIRS
                body(f, b, b, b, 0, PAIRS - 1 if b else None, start=True)
                with pe.Fori(f + 1, f + PAIRS - 2) as i:
                    body(i, b, b, b, i - f, i - (f + 1))
                body(f + PAIRS - 2, b, b, b + 1, PAIRS - 2, PAIRS - 3)
                body(f + PAIRS - 1, b, b + 1, b + 1, PAIRS - 1, PAIRS - 2)
            pe.wait_ge(t_done, STEPS)
            for n in range(4):
                if n >= 2:
                    pe.wait_ge(ptl_done[n - 2], STEPS)
                dst = wt_banks[n][:, :].bitcast(bf16)
                for t in range(8):
                    if n < 2:
                        src = w1b[:, t, n * P:(n + 1) * P]
                    else:
                        j, c = 4 * (n - 2) + t // 2, t % 2
                        src = w2b[:, c, j * P:(j + 1) * P]
                    last = pe.transpose(dst[:, t * P:(t + 1) * P], src, identb[:, :])
                last.then_inc(s_wt, 1)
            project(STEPS - 1, 1, PAIRS - 1)

            def turn_x2(b):
                pe.wait_ge(s_xn, B + b + 1)
                if b == 0:
                    pe.wait_ge(ol_done, 2 * STEPS)
                if b == 1:
                    pe.wait_ge(x1_done, B)
                if b >= 2:
                    pe.wait_ge(s_wtc[b - 2], 2)
                turn_x(x2_banks[b], b)

            turn_x2(0)
            turn_x2(1)

            def up(m):
                g, j = divmod(m, HT)
                if m == 0:
                    pe.wait_ge(s_wtc[0], 1)
                    pe.wait_ge(s_wtc[1], 1)
                if j == 0:
                    pe.wait_ge(s_tl, TURNS_C + B + 2 * (g + 1))
                if m == 2:
                    pe.wait_ge(s_wtc[0], 1)
                if m >= 3:
                    pe.wait_ge(hr_done, m - 2)
                dst = h_banks[m % 3][:, :].rearrange("p (r t) -> p r t", r=2)
                for c in range(KC):
                    w = w1T[:, c, j * P:(j + 1) * P]
                    pe.matmul(dst, w, xTh[:, 2 * g:2 * g + 2, c, :], start=c == 0, stop=False)
                    last = pe.matmul(dst, w, xTl[:, 2 * g:2 * g + 2, c, :], start=False, stop=c == KC - 1)
                last.then_inc(f1_done, 1)

            def down(m):
                g, j = divmod(m, HT)
                pe.wait_ge(sl_done, m + 1)
                if m == 0:
                    for q in s_wtc:
                        pe.wait_ge(q, 2)
                    pe.wait_ge(s_tl, TURNS_C + B + 1)
                if m == HT:
                    pe.wait_ge(s_tl, TURNS_C + 2 * B)
                for t in range(T4):
                    dst = f_banks[g][t // 2][:, (t % 2) * DIM:(t % 2 + 1) * DIM]
                    s = slice(t * P, (t + 1) * P)
                    for part in (sTh, sTl):
                        last = pe.matmul(dst, part[:, j, s], w2T[:, j, :], start=j == 0 and t % 2 == 0 and part is sTh,
                                         stop=False, skip_group_check=True)
                last.then_inc(f2_done, 1)

            def sums_f(g):
                pe.wait_ge(ha_done, HT * (g + 1))
                for t in range(T4):
                    col = g * T4 + t
                    last = pe.matmul(fs_bank[:, col:col + 1], ha[:, g, t * P:(t + 1) * P], ones[:, :], start=True, stop=True)
                last.then_inc(fs_done, 1)

            up(0)
            up(1)
            turn_x2(2)
            turn_x2(3)
            for m in range(2 * HT):
                if m + 2 < 2 * HT:
                    up(m + 2)
                down(m)
                if m == HT + 1:
                    sums_f(0)
            sums_f(1)

        @block.vector
        def _(dve):
            def ln_stats(b, call):
                ts = range(b * QT, (b + 1) * QT)
                for t in ts:
                    last = dve.bn_stats(stats[:, t, :], xt[:, t, :])
                last.then_inc(s_st, 1)
                dve.wait_ge(s_st, call)
                for t in ts:
                    last = dve.bn_aggr(mv[:, t, :], stats[:, t, :])
                last.then_inc(s_mv, 1)
                dve.wait_ge(s_mv, call)
                s = slice(b * QT, (b + 1) * QT)
                dve.tensor_scalar(lnv[:, s], mv[:, s, 1], EPS, None, ALU.add).then_inc(s_lnv, 1)

            def ln_norm(b, call):
                dve.wait_ge(s_rstd, call)
                for t in range(b * QT, (b + 1) * QT):
                    last = dve.tensor_scalar(xn[:, t, :], xt[:, t, :], mv[:, t, 0:1], rstd[:, t:t + 1],
                                             ALU.subtract, ALU.mult)
                last.then_inc(s_xn, 1)

            def low(dst, src, hi):
                return dve.tensor_tensor(dst, src, hi.bitcast(f32), ALU.subtract)

            def turned(n):
                dve.wait_ge(s_th, n + 1)
                if n < TURNS_C:
                    s = slice(4 * n, 4 * n + 4)
                    low(cTl[:, s, :].rearrange(flat3), turn_banks[n][:, :], cTh[:, s, :].rearrange(flat3)).then_inc(s_tl, 1)
                else:
                    b = n - TURNS_C
                    low(xTl[:, b, :, :].rearrange(flat3), turn_banks[n][:, :],
                        xTh[:, b, :, :].rearrange(flat3)).then_inc(s_tl, 1)

            def var_k(n):
                dve.wait_ge(ksq_done, n + 1)
                dve.tensor_reduce(ssk[:, :], ksq[:, :, :], AX.X, ALU.add).then_inc(red_done, 1)
                dve.wait_ge(red_done, n + 1)
                dve.tensor_scalar(kv[:, :], ssk[:, :], 1.0 / D, EPS, ALU.mult, ALU.add).then_inc(kv_done, 1)

            def norm_k(n):
                dve.wait_ge(rk_done, n + 1)
                dve.tensor_tensor(kn[:, :, :], bB[:, :].rearrange("p (t d) -> p t d", t=UT),
                                  rk[:, :].unsqueeze(2).broadcast_to([P, UT, D]), ALU.mult).then_inc(kn_done, 1)

            def q_lo(n):
                dve.wait_ge(qh_done, n + 1)
                low(ql[:, :, :].rearrange(flat3), bA[:, :], qh[:, :, :].rearrange(flat3)).then_inc(ql_done, 1)

            def pt_lo(i, u):
                dve.wait_ge(pth_done[u], i + 1)
                low(PTl[u][:, :, :].rearrange(flat3), bT[u][:, :], PTh[u][:, :, :].rearrange(flat3)).then_inc(ptl_done[u], 1)

            def k_lo(n):
                dve.wait_ge(kh_done, n + 1)
                dve.scalar_tensor_tensor(kl[:, :, :].rearrange(flat3), bT[1][:, :], gg[:, 0:1],
                                         kh[:, :, :].rearrange(flat3).bitcast(f32),
                                         ALU.mult, ALU.subtract).then_inc(kl_done, 1)

            def o_lo(i, u):
                dve.wait_ge(oh_done, 2 * i + u + 1)
                low(Ol[u][:, :], bO[:, u * SQ:(u + 1) * SQ], Oh[u][:, :]).then_inc(ol_done, 1)

            def var_q(n):
                dve.wait_ge(ssq_done, n + 1)
                dve.tensor_scalar(qv[:, :], bA[:, 0:UT], EPS * D, None, ALU.add).then_inc(qv_done, 1)

            def maxes(n, u):
                dve.wait_ge(s_done[u], n + 1)
                dve.tensor_reduce(mx[u][:, :], bS[u][:, :].rearrange("p (t k) -> p t k", t=QT), AX.X,
                                  ALU.max).then_inc(mx_done[u], 1)
                dve.wait_ge(mx_done[u], n + 1)
                dve.wait_ge(fq_done, n + 1)
                dve.scalar_tensor_tensor(nb[u][:, :], mx[u][:, :], -1.0, fq[:, QT * u:QT * (u + 1)],
                                         ALU.mult, ALU.mult).then_inc(nb_done[u], 1)

            def recip(n, u):
                dve.wait_ge(exp_done[u], n + 1)
                dve.reciprocal(rs[u][:, :], su[u][:, :]).then_inc(rec_done[u], 1)

            def scale_t(i):
                dve.wait_ge(t_sum, i + 1)
                if not known(i) or i >= 1:
                    dve.wait_ge(t_done, i)
                dve.tensor_scalar(gsr[:, :], gsum[:, bass.ds(SG * i, SG)], 0.5 / GROUP, CLIP,
                                  ALU.mult, ALU.max).then_inc(t_scr, 1)

            def compare_t(i):
                dve.wait_ge(t_scr, i + 1)
                w2x = wb[:, bass.ds(SG * i, SG), :]
                scale = gsr[:, :].unsqueeze(2).broadcast_to([P, SG, GROUP])
                dve.tensor_tensor(wpos[:, :, :], w2x, scale, ALU.is_gt)
                dve.scalar_tensor_tensor(wneg[:, :, :], w2x, -1.0, scale, ALU.mult, ALU.is_gt).then_inc(t_pn, 1)

            def residual(b):
                dve.wait_ge(y_done, 2 * PAIRS * (b + 1))
                dst = xt[:, QT * b:QT * (b + 1), :].rearrange(flat3)
                dve.tensor_tensor(dst, bY[:, :], dst, ALU.add).then_inc(x1_done, 1)
                dve.wait_ge(x1_done, b + 1)

            dve.wait_ge(s_x[0], 16)
            ln_stats(0, 1)
            for n in range(TURNS_C):
                turned(n)
            ln_norm(0, 1)
            dve.wait_ge(s_g, 32)
            dve.tensor_tensor(gg[:, :], gqt[:, :], gkt[:, :], ALU.mult).then_inc(s_gg, 1)
            turned(TURNS_C)
            dve.wait_ge(s_x[1], 16)
            var_k(0)
            q_lo(0)
            norm_k(0)
            for b in range(1, B):
                ln_stats(b, b + 1)
            k_lo(0)
            var_q(0)
            for b in range(1, B):
                ln_norm(b, b + 1)
            for b in range(1, B):
                turned(TURNS_C + b)
            maxes(0, 0)
            maxes(0, 1)
            var_k(1)
            recip(0, 0)
            dve.wait_ge(s_ch, 1)
            low(cl[:, :, :], ct[:, :, :], ch[:, :, :]).then_inc(s_cl, 1)
            for n in range(WWsteps):
                dve.wait_ge(s_wwh, n + 1)
                s = slice(2 * n, 2 * n + 2)
                low(WWl[:, s, :].rearrange(flat3), ww_banks[n % 4][:, :], WWh[:, s, :].rearrange(flat3)).then_inc(s_wwl, 1)

            def body(i, left=None):
                ahead = not known(i) or i + 1 < STEPS
                further = not known(i) or i + 2 < STEPS
                if ahead:
                    norm_k(i + 1)
                    q_lo(i + 1)
                recip(i, 1)
                if ahead:
                    k_lo(i + 1)
                pt_lo(i, 0)
                if left is not None:
                    residual(left)
                if ahead:
                    var_q(i + 1)
                if further:
                    var_k(i + 2)
                if ahead:
                    maxes(i + 1, 0)
                o_lo(i, 0)
                pt_lo(i, 1)
                if ahead:
                    maxes(i + 1, 1)
                scale_t(i)
                compare_t(i)
                o_lo(i, 1)
                if ahead:
                    recip(i + 1, 0)
                if left is not None:
                    ln_stats(left, B + left + 1)

            for b in range(B):
                f = b * PAIRS
                body(f, left=b - 1 if b else None)
                end = f + PAIRS if b < B - 1 else STEPS - 2
                with dve.Fori(f + 1, end) as i:
                    body(i)
                if b:
                    ln_norm(b - 1, B + b)
            body(STEPS - 2)
            body(STEPS - 1)

            def weights(n):
                dve.wait_ge(s_wt, n + 1)
                dve.tensor_copy((w1T[:, n, :] if n < 2 else w2T[:, 4 * (n - 2):4 * (n - 2) + 4, :].rearrange(flat3)),
                                wt_banks[n][:, :].bitcast(bf16)).then_inc(s_wtc[1], 1)

            def turned_2(b):
                dve.wait_ge(s_th, TURNS_C + B + b + 1)
                low(xTl[:, b, :, :].rearrange(flat3), x2_banks[b][:, :], xTh[:, b, :, :].rearrange(flat3)).then_inc(s_tl, 1)

            weights(1)
            residual(B - 1)
            turned_2(0)
            turned_2(1)
            weights(3)
            ln_stats(B - 1, 2 * B)
            ln_norm(B - 1, 2 * B)

            def finish(g):
                dve.wait_ge(fs_done, g + 1)
                dve.tensor_scalar(fv[:, g * T4:(g + 1) * T4], fs_bank[:, g * T4:(g + 1) * T4], 1.0 / HID, EPS_F,
                                  ALU.mult, ALU.add).then_inc(fv_done, 1)
                dve.wait_ge(fr_done, g + 1)
                dve.wait_ge(f2_done, HT * (g + 1))
                for t in range(T4):
                    src = f_banks[g][t // 2][:, (t % 2) * DIM:(t % 2 + 1) * DIM]
                    n = g * T4 + t
                    last = dve.scalar_tensor_tensor(yo[:, n, :], src, fr[:, n:n + 1], xt[:, n, :], ALU.mult, ALU.add)
                    if t % 2:
                        last.then_inc(yo_done, 1)

            for m in range(2 * HT):
                g, j = divmod(m, HT)
                if m == 2:
                    turned_2(2)
                    turned_2(3)
                dve.wait_ge(hs_done, m + 1)
                if g == 1:
                    dve.wait_ge(f2_done, j + 1)
                dve.tensor_copy(sTh[:, j, :], hs[m % 2]).then_inc(sh_done, 1)
                dve.wait_ge(sh_done, m + 1)
                low(sTl[:, j, :], hs[m % 2], sTh[:, j, :]).then_inc(sl_done, 1)
                if m == HT + 2:
                    finish(0)
            finish(1)


_INS = ['x', 'ctx_1024', 'L0_xattn_Wq', 'L0_xattn_Wk', 'L0_xattn_Wv', 'L0_xattn_Wo', 'L0_xattn_gq', 'L0_xattn_gk',
        'L0_ffn_W_fc', 'L0_ffn_W_proj']


def kernel(**inputs):
    import numpy as np
    import concourse.bacc as bacc
    from concourse import mybir
    from concourse.bass_utils import run_bass_kernel_spmd

    nc = bacc.Bacc("TRN2", target_bir_lowering=False, num_devices=1)
    arrays, args = {}, []
    for name in _INS:
        a = np.ascontiguousarray(inputs[name])
        arrays[f"in_{name}"] = a
        args.append(nc.dram_tensor(f"in_{name}", a.shape, mybir.dt.from_np(a.dtype), kind="ExternalInput").ap())
    args.append(nc.dram_tensor("out", arrays["in_x"].shape, mybir.dt.float32, kind="ExternalOutput").ap())
    xattn_ffn(nc, *args)
    r = run_bass_kernel_spmd(nc, [arrays], core_ids=[0])
    return r.results[0]["out"]
```

```python
import concourse.bass as bass
from concourse import mybir
from contextlib import ExitStack


def xattn_ffn(nc, x, ctx, Wq, Wk, Wv, Wo, gq, gk, W_fc, W_proj, out):
    f32 = mybir.dt.float32
    f32r = mybir.dt.float32r
    bf16 = mybir.dt.bfloat16
    ALU = mybir.AluOpType
    ACT = mybir.ActivationFunctionType
    AX = mybir.AxisListType

    P = 128
    B, SQ, DIM = x.shape
    SKV, CD = ctx.shape[1:]
    D = gq.shape[0]
    H = Wq.shape[1] // D
    HID = W_fc.shape[0]
    GROUP = 64
    NT = B * SQ // P
    KC = DIM // P
    HT = HID // P
    HALF = B * SQ // 2
    QT = SQ // P
    KT = SKV // P
    T4 = HALF // P
    PAIRS = H // 2
    STEPS = B * PAIRS
    UT = 2 * KT
    NG = 2 * KC * HID // GROUP
    SG = NG // STEPS
    EPS = 1e-5
    EPS_F = 2.0 ** -23
    CLIP = 1.00117176771164e-08

    x_v = x.rearrange("b (t p) d -> p (b t) d", p=P)
    ctx_v = ctx.rearrange("b (t p) d -> p (b t) d", p=P)
    out_v = out.rearrange("b (t p) d -> p (b t) d", p=P)
    flat3 = "p a b -> p (a b)"

    es = ExitStack()
    with es:
        def sb(name, shape, dt=f32):
            return es.enter_context(nc.sbuf_tensor(name, shape, dt))

        def sem(name):
            return es.enter_context(nc.semaphore(name))

        xt = sb("xt", [P, NT, DIM])
        ct = sb("ct", [P, NT, CD])
        Wqr = sb("Wqr", [P, KC, 2, D])
        Wkr = sb("Wkr", [P, 2, D])
        Wvr = sb("Wvr", [P, H, D])
        Wor = sb("Wor", [P, H, DIM])
        gqt = sb("gqt", [P, 1])
        gkt = sb("gkt", [P, 1])
        gg = sb("gg", [P, 1])
        fpr = sb("fpr", [P, NG, GROUP])
        ident = sb("ident", [P, P])
        identb = sb("identb", [P, P], bf16)
        ones = sb("ones", [P, 1])
        mhalf = sb("mhalf", [P, NT])
        stats = sb("stats", [P, NT, 6])
        mv = sb("mv", [P, NT, 2])
        lnv = sb("lnv", [P, NT])
        rstd = sb("rstd", [P, NT])
        xn = sb("xn", [P, NT, DIM])
        xTh = sb("xTh", [P, B, KC, SQ], f32r)
        xTl = sb("xTl", [P, B, KC, SQ], f32r)
        cTh = sb("cTh", [P, NT, P], f32r)
        cTl = sb("cTl", [P, NT, P], f32r)
        ch = sb("ch", [P, NT, CD], f32r)
        cl = sb("cl", [P, NT, CD], f32r)
        WvT = sb("WvT", [P, H, CD])
        WWh = sb("WWh", [P, H, DIM], f32r)
        WWl = sb("WWl", [P, H, DIM], f32r)
        wb = Wvr[:, :, :].rearrange(flat3).bitcast(bf16).rearrange("p (n k) -> p n k", k=GROUP)
        wabs = sb("wabs", [P, SG, GROUP], bf16)
        gsum = sb("gsum", [P, NG])
        gsr = sb("gsr", [P, SG], bf16)
        wpos = sb("wpos", [P, SG, GROUP], bf16)
        wneg = sb("wneg", [P, SG, GROUP], bf16)
        wt = Wor[:, 0:H // 2, :].rearrange(flat3).bitcast(bf16).rearrange("p (n k) -> p n k", k=GROUP)
        w1b = wt[:, 0:NG // 2, :].rearrange(flat3).rearrange("p (j d) -> p j d", j=HT)
        w2b = wt[:, NG // 2:NG, :].rearrange(flat3).rearrange("p (c h) -> p c h", c=KC)
        w1T = sb("w1T", [P, KC, HID], f32r)
        w2T = sb("w2T", [P, HT, DIM], f32r)
        Wqh = sb("Wqh", [P, KC, 2, D], f32r)
        Wql = sb("Wql", [P, KC, 2, D], f32r)
        Wkh = sb("Wkh", [P, 2, D], f32r)
        Wkl = sb("Wkl", [P, 2, D], f32r)
        ksq = sb("ksq", [P, UT, D])
        ssk = sb("ssk", [P, UT])
        kv = sb("kv", [P, UT])
        rk = sb("rk", [P, UT])
        kn = sb("kn", [P, UT, D])
        kh = sb("kh", [P, 2, SKV], f32r)
        kl = sb("kl", [P, 2, SKV], f32r)
        qsq = sb("qsq", [P, 2, SQ])
        qh = sb("qh", [P, 2, SQ], f32r)
        ql = sb("ql", [P, 2, SQ], f32r)
        qv = sb("qv", [P, UT])
        fq = sb("fq", [P, UT])
        mx = [sb(f"mx{u}", [P, QT]) for u in range(2)]
        nb = [sb(f"nb{u}", [P, QT]) for u in range(2)]
        su = [sb(f"su{u}", [P, QT]) for u in range(2)]
        rs = [sb(f"rs{u}", [P, QT]) for u in range(2)]
        Pr = [sb(f"Pr{u}", [P, QT, SKV]) for u in range(2)]
        PTh = [sb(f"PTh{u}", [P, KT, SQ], f32r) for u in range(2)]
        PTl = [sb(f"PTl{u}", [P, KT, SQ], f32r) for u in range(2)]
        Oh = [sb(f"Oh{u}", [P, SQ], f32r) for u in range(2)]
        Ol = [sb(f"Ol{u}", [P, SQ], f32r) for u in range(2)]
        hr = [Pr[0][:, :, :].rearrange(flat3), Pr[1][:, :, :].rearrange(flat3)]
        hs = [kn[:, :, :].rearrange(flat3), ksq[:, :, :].rearrange(flat3), WvT[:, 0:4, :].rearrange(flat3)]
        h4 = [qsq[:, :, :].rearrange(flat3), Wor[:, H // 2:H // 2 + 2, :].rearrange(flat3),
              Wor[:, H // 2 + 2:H // 2 + 4, :].rearrange(flat3)]
        ha = ct[:, :, :].rearrange(flat3).rearrange("p (g t) -> p g t", g=2)
        fv = sb("fv", [P, NT])
        fr = sb("fr", [P, NT])
        yo = xn

        def bank(name):
            return es.enter_context(nc.psum_tensor(name, [P, 512], f32))

        bA = bank("bA")
        bB = bank("bB")
        bS = [bank("bS0"), bank("bS1")]
        bT = [bank("bT0"), bank("bT1")]
        bO = bank("bO")
        bY = bank("bY")

        s_x = [sem("s_x0"), sem("s_x1")]; s_c = sem("s_c"); s_g = sem("s_g"); s_wq = sem("s_wq"); s_wk = sem("s_wk")
        s_wv = sem("s_wv"); s_wo = [sem("s_wo0"), sem("s_wo1")]; s_ffn = sem("s_ffn")
        s_out = sem("s_out")
        s_own = sem("s_own"); s_const0 = sem("s_const0"); s_const = sem("s_const")
        s_mh = sem("s_mh"); s_gg = sem("s_gg")
        s_st = sem("s_st"); s_mv = sem("s_mv"); s_lnv = sem("s_lnv"); s_rstd = sem("s_rstd"); s_xn = sem("s_xn")
        s_turn = sem("s_turn")
        s_th = sem("s_th"); s_tl = sem("s_tl")
        s_ch = sem("s_ch"); s_cl = sem("s_cl")
        s_wvT = sem("s_wvT"); s_wvc = sem("s_wvc")
        s_ww = sem("s_ww"); s_wwh = sem("s_wwh"); s_wwl = sem("s_wwl")
        t_wb = sem("t_wb"); t_sum = sem("t_sum"); t_scr = sem("t_scr")
        t_pn = sem("t_pn"); t_dif = sem("t_dif"); t_done = sem("t_done")
        s_wt = sem("s_wt"); s_wtc = [sem("s_wtc0"), sem("s_wtc1")]
        wqh_done = sem("wqh_done"); wq_done = sem("wq_done"); wkh_done = sem("wkh_done"); wk_done = sem("wk_done")
        k_done = sem("k_done"); q_done = sem("q_done"); kt_done = sem("kt_done"); ssq_done = sem("ssq_done")
        s_done = [sem("s_done0"), sem("s_done1")]
        pt_done = [sem("pt_done0"), sem("pt_done1")]
        av_done = sem("av_done"); y_done = sem("y_done")
        ksq_done = sem("ksq_done"); qsq_done = sem("qsq_done"); qh_done = sem("qh_done")
        pth_done = [sem("pth_done0"), sem("pth_done1")]
        kh_done = sem("kh_done"); oh_done = sem("oh_done")
        exp_done = [sem("exp_done0"), sem("exp_done1")]
        red_done = sem("red_done"); kv_done = sem("kv_done"); kn_done = sem("kn_done"); ql_done = sem("ql_done")
        ptl_done = [sem("ptl_done0"), sem("ptl_done1")]
        kl_done = sem("kl_done"); ol_done = sem("ol_done"); qv_done = sem("qv_done")
        mx_done = [sem("mx_done0"), sem("mx_done1")]
        nb_done = [sem("nb_done0"), sem("nb_done1")]
        rec_done = [sem("rec_done0"), sem("rec_done1")]
        pn_done = [sem("pn_done0"), sem("pn_done1")]
        rk_done = sem("rk_done"); fq_done = sem("fq_done"); x1_done = sem("x1_done")
        f1_done = sem("f1_done"); hr_done = sem("hr_done"); hs_done = sem("hs_done")
        sh_done = sem("sh_done"); sl_done = sem("sl_done"); h4_done = sem("h4_done"); ha_done = sem("ha_done")
        f2_done = sem("f2_done"); fs_done = sem("fs_done"); fv_done = sem("fv_done"); fr_done = sem("fr_done")
        yo_done = sem("yo_done")

        WARM = 16
        WWsteps = H // 2
        TURNS_C = NT * CD // 512
        turn_banks = [bS[0], bS[1], bT[0], bY, bS[0], bS[1]]
        wv_banks = [bS[0], bS[1], bT[0], bO]
        ww_banks = [bT[0], bO, bT[1], bY]
        wt_banks = [bA, bB, bS[0], bS[1]]
        x2_banks = [bS[0], bS[1], bT[0], bT[1]]
        sTh = WWh[:, :, :].rearrange(flat3).rearrange("p (j t) -> p j t", j=HT)
        sTl = WWl[:, :, :].rearrange(flat3).rearrange("p (j t) -> p j t", j=HT)
        h_banks = [bA, bB, bO]
        f_banks = [[bS[0], bS[1]], [bY, bT[0]]]
        fs_bank = bT[1]

        def known(n):
            return isinstance(n, int)

        block = es.enter_context(nc.Block())

        @block.sync
        def _(sp):
            def load_k(n, pair):
                if not known(n) or n >= 1:
                    sp.wait_ge(wk_done, n)
                sp.dma_start(Wkr[:, :, :].rearrange(flat3), Wk[:, bass.ds(2 * D * pair, 2 * D)]).then_inc(s_wk, 16)

            def load_q(n, pair):
                if not known(n) or n >= 1:
                    sp.wait_ge(wq_done, n)
                sp.dma_start(Wqr[:, :, :, :].rearrange("p c u d -> p c (u d)"),
                             Wq.rearrange("(c p) n -> p c n", p=P)[:, :, bass.ds(2 * D * pair, 2 * D)]).then_inc(s_wq, 16)

            sp.dma_start(xt[:, 0:QT, :], x_v[:, 0:QT, :]).then_inc(s_x[0], 16)
            sp.dma_start(ct[:, :, :], ctx_v).then_inc(s_c, 16)
            load_k(0, 0)
            load_q(0, 0)
            sp.dma_start(xt[:, QT:NT, :], x_v[:, QT:NT, :]).then_inc(s_x[1], 16)
            sp.dma_start(Wvr[:, :, :], Wv.rearrange("p (h d) -> p h d", d=D)).then_inc(s_wv, 16)
            for m in range(2):
                hs_ = slice(m * H // 2, (m + 1) * H // 2)
                sp.dma_start(Wor[:, hs_, :], Wo.rearrange("(h p) n -> p h n", p=P)[:, hs_, :]).then_inc(s_wo[m], 16)
                if m == 0:
                    load_k(1, 1)
                    load_q(1, 1)
            sp.dma_start(fpr[:, 0:NG // 2, :].rearrange(flat3).rearrange("p (j d) -> p j d", j=HT),
                         W_fc.rearrange("(j p) d -> p j d", p=P)).then_inc(s_ffn, 16)
            sp.dma_start(fpr[:, NG // 2:NG, :].rearrange(flat3).rearrange("p (t h) -> p t h", t=KC),
                         W_proj.rearrange("(t p) h -> p t h", p=P)).then_inc(s_ffn, 16)
            for b in range(B):
                f = b * PAIRS
                with sp.Fori(f + (0 if b else 2), f + PAIRS) as n:
                    load_k(n, n - f)
                    load_q(n, n - f)
            for n in range(4):
                sp.wait_ge(yo_done, n + 1)
                sp.dma_start(out_v[:, 2 * n:2 * n + 2, :], yo[:, 2 * n:2 * n + 2, :]).then_inc(s_out, 16)
            sp.wait_ge(s_out, 64)

        @block.gpsimd
        def _(gp):
            gp.memset(mhalf[:, :], -0.5).then_inc(s_mh, 1)
            gp.memset(ones[:, :], 1.0).then_inc(s_const, 1)
            gp.memset(ident[:, :], 0.0).then_inc(s_const0, 1)
            gp.memset(identb[:, :], 0.0).then_inc(s_const0, 1)
            gp.wait_ge(s_const0, 2)
            for m in (ident, identb):
                gp.affine_select(out=m[:, :], in_=m[:, :], compare_op=ALU.not_equal, fill=1.0,
                                 base=0, pattern=[[-1, P]], channel_multiplier=1).then_inc(s_const, 1)
            gp.wait_ge(s_mh, 1)

            def split(n, src, loaded, hi, lo, used, hi_done, done):
                if not known(n) or n >= 1:
                    gp.wait_ge(used, n)
                gp.wait_ge(loaded, 16 * (n + 1))
                gp.sem_inc(s_own, 1)
                gp.tensor_scalar(hi, src, 1.0, 1.0, ALU.mult, ALU.mult).then_inc(hi_done, 1)
                gp.wait_ge(hi_done, n + 1)
                gp.sem_inc(s_own, 1)
                gp.tensor_tensor(lo, src, hi.bitcast(f32), ALU.subtract).then_inc(done, 1)

            def split_q(n):
                flat = "p c u d -> p (c u d)"
                split(n, Wqr[:, :, :, :].rearrange(flat), s_wq, Wqh[:, :, :, :].rearrange(flat),
                      Wql[:, :, :, :].rearrange(flat), q_done, wqh_done, wq_done)

            def split_k(n):
                split(n, Wkr[:, :, :].rearrange(flat3), s_wk, Wkh[:, :, :].rearrange(flat3),
                      Wkl[:, :, :].rearrange(flat3), k_done, wkh_done, wk_done)

            def rsqrt_k(n):
                gp.wait_ge(red_done, n + 1)
                gp.sem_inc(s_own, 1)
                gp.tensor_scalar(kv[:, :], ssk[:, :], 1.0 / D, EPS, ALU.mult, ALU.add).then_inc(kv_done, 1)
                gp.wait_ge(kv_done, n + 1)
                gp.tensor_tensor(rk[:, :], kv[:, :], mhalf[:, 0:UT], ALU.pow).then_inc(rk_done, 1)

            def rsqrt_q(n):
                gp.wait_ge(qv_done, n + 1)
                gp.tensor_tensor(fq[:, :], qv[:, :], mhalf[:, 0:UT], ALU.pow).then_inc(fq_done, 1)

            def rsqrt_ln(call, b, rows=1):
                s = slice(b * QT, (b + rows) * QT)
                gp.wait_ge(s_lnv, call)
                gp.tensor_tensor(rstd[:, s], lnv[:, s], mhalf[:, 0:QT * rows], ALU.pow).then_inc(s_rstd, 1)

            def norm_p(n):
                gp.wait_ge(rec_done[0], n + 1)
                gp.sem_inc(s_own, 1)
                for t in range(QT):
                    last = gp.tensor_scalar(Pr[0][:, t, :], Pr[0][:, t, :], rs[0][:, t:t + 1], 1.0,
                                            ALU.mult, ALU.mult)
                last.then_inc(pn_done[0], 1)

            def ternary(i):
                gp.wait_ge(t_pn, i + 1)
                gp.tensor_tensor(wpos[:, :, :], wpos[:, :, :], wneg[:, :, :], ALU.subtract).then_inc(t_dif, 1)
                gp.wait_ge(t_dif, i + 1)
                gp.sem_inc(s_own, 1)
                gp.tensor_tensor(wt[:, bass.ds(SG * i, SG), :], wpos[:, :, :],
                                 gsr[:, :].unsqueeze(2).broadcast_to([P, SG, GROUP]), ALU.mult).then_inc(t_done, 1)

            rsqrt_ln(1, 0)
            split_k(0)
            split_q(0)
            rsqrt_ln(2, 1, B - 1)
            rsqrt_k(0)
            split_k(1)
            split_q(1)
            gp.wait_ge(s_ch, 1)
            gp.tensor_tensor(cl[:, :, :], ct[:, :, :], ch[:, :, :].bitcast(f32), ALU.subtract).then_inc(s_cl, 1)
            rsqrt_q(0)
            rsqrt_k(1)
            norm_p(0)
            split_k(2)

            def body(i, ln=None):
                if not known(i) or i + 3 < STEPS:
                    split_k(i + 3)
                if not known(i) or i + 1 < STEPS:
                    rsqrt_q(i + 1)
                if not known(i) or i + 2 < STEPS:
                    split_q(i + 2)
                    rsqrt_k(i + 2)
                if not known(i) or i + 1 < STEPS:
                    norm_p(i + 1)
                ternary(i)
                if ln is not None:
                    rsqrt_ln(ln + 3, ln)

            for b in range(B):
                f = b * PAIRS
                if b:
                    for i in range(f, f + 3):
                        body(i, ln=b - 1 if i == f + 2 else None)
                with gp.Fori(f + 3 if b else 0, f + PAIRS if b < B - 1 else STEPS - 3) as i:
                    body(i)
            for i in range(STEPS - 3, STEPS):
                body(i)

            rsqrt_ln(B + 2, B - 1)

            def rsqrt_f(g):
                gp.wait_ge(fv_done, g + 1)
                gp.tensor_tensor(fr[:, g * T4:(g + 1) * T4], fv[:, g * T4:(g + 1) * T4], mhalf[:, 0:T4],
                                 ALU.pow).then_inc(fr_done, 1)

            for m in range(2 * HT - 1):
                g, j = divmod(m, HT)
                gp.wait_ge(h4_done, m + 1)
                if j == 0:
                    gp.tensor_scalar(ha[:, g, :], h4[m % 3], 1.0, 1.0, ALU.mult, ALU.mult).then_inc(ha_done, 1)
                else:
                    gp.wait_ge(ha_done, m)
                    gp.tensor_tensor(ha[:, g, :], ha[:, g, :], h4[m % 3], ALU.add).then_inc(ha_done, 1)
                if m == HT + 3:
                    rsqrt_f(0)
            rsqrt_f(1)

        @block.scalar
        def _(act):
            act.dma_start(gqt[:, :], gq.rearrange("(p o) -> p o", o=1)).then_inc(s_g, 16)
            act.dma_start(gkt[:, :], gk.rearrange("(p o) -> p o", o=1)).then_inc(s_g, 16)

            def turned(n):
                act.wait_ge(s_turn, n + 1)
                if n < TURNS_C:
                    dst = cTh[:, 4 * n:4 * n + 4, :]
                else:
                    dst = xTh[:, n - TURNS_C, :, :]
                act.activation(dst.rearrange(flat3), turn_banks[n][:, :], ACT.Copy).then_inc(s_th, 1)

            def k_square(n):
                act.wait_ge(k_done, n + 1)
                act.activation(ksq[:, :, :].rearrange(flat3), bB[:, :], ACT.Square).then_inc(ksq_done, 1)

            def q_parts(n):
                act.wait_ge(q_done, n + 1)
                act.activation(qsq[:, :, :].rearrange(flat3), bA[:, :], ACT.Square).then_inc(qsq_done, 1)
                act.activation(qh[:, :, :].rearrange(flat3), bA[:, :], ACT.Copy).then_inc(qh_done, 1)

            def pt_hi(i, u):
                act.wait_ge(pt_done[u], i + 1)
                act.activation(PTh[u][:, :, :].rearrange(flat3), bT[u][:, :], ACT.Copy).then_inc(pth_done[u], 1)

            def k_hi(n):
                act.wait_ge(kt_done, n + 1)
                act.activation(kh[:, :, :].rearrange(flat3), bT[1][:, :], ACT.Copy, scale=gg[:, 0:1]).then_inc(kh_done, 1)

            def o_hi(i, u):
                act.wait_ge(av_done, 2 * i + u + 1)
                act.activation(Oh[u][:, :], bO[:, u * SQ:(u + 1) * SQ], ACT.Copy).then_inc(oh_done, 1)

            def exps(n, u):
                act.wait_ge(nb_done[u], n + 1)
                for t in range(QT):
                    last = act.activation(Pr[u][:, t, :], bS[u][:, t * SKV:(t + 1) * SKV], ACT.Exp,
                                          bias=nb[u][:, t:t + 1], scale=fq[:, QT * u + t:QT * u + t + 1],
                                          accum_out=su[u][:, t:t + 1])
                last.then_inc(exp_done[u], 1)

            def norm_p(i):
                act.wait_ge(rec_done[1], i + 1)
                for t in range(QT):
                    last = act.activation(Pr[1][:, t, :], Pr[1][:, t, :], ACT.Copy, scale=rs[1][:, t:t + 1])
                last.then_inc(pn_done[1], 1)

            def ternary(i):
                act.wait_ge(s_ffn, 32)
                act.activation(wb[:, bass.ds(SG * i, SG), :].rearrange(flat3),
                               fpr[:, bass.ds(SG * i, SG), :].rearrange(flat3), ACT.Copy, scale=2.0).then_inc(t_wb, 1)
                act.wait_ge(t_wb, i + 1)
                for k in range(SG):
                    last = act.activation(wabs[:, k, :], wb[:, bass.ds(SG * i + k, 1), :].rearrange(flat3), ACT.Abs,
                                          accum_out=gsum[:, bass.ds(SG * i + k, 1)])
                last.then_inc(t_sum, 1)

            def wv_copy(n):
                act.wait_ge(s_wvT, n + 1)
                act.activation(WvT[:, 4 * n:4 * n + 4, :].rearrange(flat3), wv_banks[n][:, :], ACT.Copy).then_inc(s_wvc, 1)

            def ww_hi(n):
                act.wait_ge(s_ww, n + 1)
                act.activation(WWh[:, 2 * n:2 * n + 2, :].rearrange(flat3), ww_banks[n % 4][:, :],
                               ACT.Copy).then_inc(s_wwh, 1)

            act.wait_ge(s_c, 16)
            act.activation(ch[:, :, :], ct[:, :, :], ACT.Copy).then_inc(s_ch, 1)
            for n in range(TURNS_C + 1):
                turned(n)
            k_square(0)
            q_parts(0)
            for n in range(H // 4):
                wv_copy(n)
            ww_hi(0)
            act.wait_ge(s_gg, 1)
            k_hi(0)
            ww_hi(1)
            for n in range(TURNS_C + 1, TURNS_C + B):
                turned(n)
            ww_hi(2)
            k_square(1)
            ww_hi(3)
            exps(0, 0)
            ww_hi(4)
            ww_hi(5)
            exps(0, 1)
            ww_hi(6)
            ww_hi(7)

            def body(i):
                ahead = not known(i) or i + 1 < STEPS
                if ahead:
                    q_parts(i + 1)
                    k_hi(i + 1)
                pt_hi(i, 0)
                if not known(i) or i + 2 < STEPS:
                    k_square(i + 2)
                norm_p(i)
                ternary(i)
                o_hi(i, 0)
                pt_hi(i, 1)
                if ahead:
                    exps(i + 1, 0)
                if known(i):
                    ternary(i + 1)
                o_hi(i, 1)
                if ahead:
                    exps(i + 1, 1)

            with act.Fori(0, STEPS - 2) as i:
                body(i)
            body(STEPS - 2)

            def weights(n):
                act.wait_ge(s_wt, n + 1)
                act.activation((w1T[:, n, :] if n < 2 else w2T[:, 4 * (n - 2):4 * (n - 2) + 4, :].rearrange(flat3)),
                               wt_banks[n][:, :].bitcast(bf16), ACT.Copy).then_inc(s_wtc[0], 1)

            def turned_2(b):
                act.wait_ge(s_turn, TURNS_C + B + b + 1)
                act.activation(xTh[:, b, :, :].rearrange(flat3), x2_banks[b][:, :], ACT.Copy).then_inc(s_th, 1)

            def relu(m):
                act.wait_ge(f1_done, m + 1)
                if m >= 2:
                    act.wait_ge(hs_done, m - 1)
                act.activation(hr[m % 2], h_banks[m % 3][:, :], ACT.Relu).then_inc(hr_done, 1)

            def hidden(m):
                g, j = divmod(m, HT)
                act.wait_ge(hs_done, m + 1)
                if g == 1:
                    act.wait_ge(f2_done, j + 1)
                if m == HT - 1:
                    act.wait_ge(y_done, 2 * STEPS)
                act.activation(sTh[:, j, :], hs[m % 3], ACT.Copy).then_inc(sh_done, 1)
                if m >= 3:
                    act.wait_ge(ha_done, m - 2)
                act.activation(h4[m % 3], hs[m % 3], ACT.Square).then_inc(h4_done, 1)

            last = STEPS - 1
            norm_p(last)
            pt_hi(last, 0)
            weights(0)
            pt_hi(last, 1)
            turned_2(0)
            turned_2(1)
            o_hi(last, 0)
            weights(2)
            relu(0)
            o_hi(last, 1)
            relu(1)
            for m in range(2 * HT):
                hidden(m)
                if m + 2 < 2 * HT:
                    relu(m + 2)
                if m == 3:
                    turned_2(2)
                    turned_2(3)

        @block.tensor
        def _(pe):
            def three(dst, sth, stl, mvh, mvl, start, stop, **kw):
                pe.matmul(dst, sth, mvh, start=start, stop=False, **kw)
                pe.matmul(dst, sth, mvl, start=False, stop=False, **kw)
                return pe.matmul(dst, stl, mvh, start=False, stop=stop, **kw)

            def turn_x(dst, b):
                for c in range(KC):
                    for t in range(QT):
                        last = pe.transpose(dst[:, (QT * c + t) * P:(QT * c + t + 1) * P],
                                            xn[:, QT * b + t, c * P:(c + 1) * P], ident[:, :])
                last.then_inc(s_turn, 1)

            def keys(n, b):
                pe.wait_ge(wk_done, n + 1)
                if not known(n) or n >= 1:
                    pe.wait_ge(kn_done, n)
                for t in range(KT):
                    last = three(bB[:, t * 2 * D:(t + 1) * 2 * D], cTh[:, KT * b + t, :], cTl[:, KT * b + t, :],
                                 Wkh[:, :, :].rearrange(flat3), Wkl[:, :, :].rearrange(flat3), True, True)
                last.then_inc(k_done, 1)

            def queries(n, b):
                pe.wait_ge(wq_done, n + 1)
                if not known(n) or n >= 1:
                    pe.wait_ge(qv_done, n)
                for u in range(2):
                    for c in range(KC):
                        last = three(bA[:, u * SQ:(u + 1) * SQ], Wqh[:, c, u, :], Wql[:, c, u, :],
                                     xTh[:, b, c, :], xTl[:, b, c, :], c == 0, c == KC - 1)
                last.then_inc(q_done, 1)

            def turn_p(i, u):
                pe.wait_ge(pn_done[u], i + 1)
                if u == 1 and (not known(i) or i + 1 < STEPS):
                    pe.wait_ge(kl_done, i + 2)
                elif not known(i) or i >= 1:
                    pe.wait_ge(ptl_done[u], i)
                for t in range(QT):
                    for k in range(KT):
                        last = pe.transpose(bT[u][:, k * SQ + t * P:k * SQ + (t + 1) * P],
                                            Pr[u][:, t, k * P:(k + 1) * P], ident[:, :])
                last.then_inc(pt_done[u], 1)

            def turn_k(n):
                pe.wait_ge(kn_done, n + 1)
                if not known(n) or n >= 2:
                    pe.wait_ge(ptl_done[1], n - 1)
                for t in range(KT):
                    for u in range(2):
                        last = pe.transpose(bT[1][:, u * SKV + t * P:u * SKV + (t + 1) * P], kn[:, 2 * t + u, :], ident[:, :])
                last.then_inc(kt_done, 1)

            def project(i, u, pair, start=False):
                pe.wait_ge(ol_done, 2 * i + u + 1)
                for t in range(QT):
                    s = slice(t * P, (t + 1) * P)
                    last = three(bY[:, t * DIM:(t + 1) * DIM], Oh[u][:, s], Ol[u][:, s],
                                 WWh[:, bass.ds(2 * pair + u, 1), :].rearrange(flat3),
                                 WWl[:, bass.ds(2 * pair + u, 1), :].rearrange(flat3),
                                 start and t == 0, False, skip_group_check=True)
                last.then_inc(y_done, 1)

            def attend(i, u, b):
                pe.wait_ge(ptl_done[u], i + 1)
                for k in range(KT):
                    last = three(bO[:, u * SQ:(u + 1) * SQ], ch[:, KT * b + k, :], cl[:, KT * b + k, :],
                                 PTh[u][:, k, :], PTl[u][:, k, :], k == 0, k == KT - 1)
                last.then_inc(av_done, 1)

            def sums_q(n):
                pe.wait_ge(qsq_done, n + 1)
                pe.wait_ge(ql_done, n + 1)
                for j in range(UT):
                    u, t = divmod(j, QT)
                    last = pe.matmul(bA[:, j:j + 1], qsq[:, u, t * P:(t + 1) * P], ones[:, :], start=True, stop=True)
                last.then_inc(ssq_done, 1)

            def scores(n, u):
                pe.wait_ge(kl_done, n + 1)
                if not known(n) or n >= 1:
                    pe.wait_ge(exp_done[u], n)
                for t in range(QT):
                    s = slice(t * P, (t + 1) * P)
                    last = three(bS[u][:, t * SKV:(t + 1) * SKV], qh[:, u, s], ql[:, u, s], kh[:, u, :], kl[:, u, :],
                                 True, True)
                last.then_inc(s_done[u], 1)

            pe.wait_ge(s_const, 3)
            for _ in range(WARM):
                pe.transpose(bA[:, 0:P], ident[:, :], ident[:, :])
            pe.wait_ge(s_c, 16)
            for n in range(TURNS_C):
                for t in range(4):
                    last = pe.transpose(turn_banks[n][:, t * P:(t + 1) * P], ct[:, 4 * n + t, :], ident[:, :])
                last.then_inc(s_turn, 1)
            pe.wait_ge(s_xn, 1)
            turn_x(turn_banks[TURNS_C], 0)
            pe.wait_ge(s_tl, TURNS_C)
            keys(0, 0)
            pe.wait_ge(s_tl, TURNS_C + 1)
            queries(0, 0)
            pe.wait_ge(s_wv, 16)
            for n in range(H // 4):
                for t in range(4):
                    last = pe.transpose(wv_banks[n][:, t * P:(t + 1) * P], Wvr[:, 4 * n + t, :], ident[:, :])
                last.then_inc(s_wvT, 1)

            def wv_wo(n):
                if n % 4 == 0:
                    pe.wait_ge(s_wo[n // 4], 16)
                if n == 0:
                    pe.wait_ge(s_wvc, 4)
                if n == 2:
                    pe.wait_ge(kl_done, 1)
                if n == 3:
                    pe.wait_ge(s_tl, TURNS_C + 2)
                if n >= 4:
                    pe.wait_ge(s_wwl, n - 3)
                for t in range(2):
                    last = pe.matmul(ww_banks[n % 4][:, t * DIM:(t + 1) * DIM], WvT[:, 2 * n + t, :],
                                     Wor[:, 2 * n + t, :], start=True, stop=True)
                last.then_inc(s_ww, 1)

            wv_wo(0)
            turn_k(0)
            wv_wo(1)
            sums_q(0)
            for b in range(1, B):
                pe.wait_ge(s_xn, b + 1)
                turn_x(turn_banks[TURNS_C + b], b)
            wv_wo(2)
            keys(1, 0)
            wv_wo(3)
            pe.wait_ge(s_tl, TURNS_C + B)
            scores(0, 0)
            scores(0, 1)
            for n in range(4, WWsteps):
                wv_wo(n)

            def body(i, b, bn, bm, pair, before, start=False):
                ahead = not known(i) or i + 1 < STEPS
                if ahead:
                    queries(i + 1, bn)
                if known(i) and i == 0:
                    pe.wait_ge(s_wwl, WWsteps - 1)
                    pe.wait_ge(s_cl, 1)
                if before is not None:
                    project(i - 1, 1, before)
                if ahead:
                    turn_k(i + 1)
                turn_p(i, 0)
                if not known(i) or i + 2 < STEPS:
                    keys(i + 2, bm)
                if ahead:
                    sums_q(i + 1)
                    scores(i + 1, 0)
                attend(i, 0, b)
                turn_p(i, 1)
                if ahead:
                    scores(i + 1, 1)
                if start and b:
                    pe.wait_ge(x1_done, b)
                elif start:
                    pe.wait_ge(s_wwl, WWsteps)
                project(i, 0, pair, start)
                attend(i, 1, b)

            for b in range(B):
                f = b * PAIRS
                body(f, b, b, b, 0, PAIRS - 1 if b else None, start=True)
                with pe.Fori(f + 1, f + PAIRS - 2) as i:
                    body(i, b, b, b, i - f, i - (f + 1))
                body(f + PAIRS - 2, b, b, b + 1, PAIRS - 2, PAIRS - 3)
                if b < B - 1:
                    body(f + PAIRS - 1, b, b + 1, b + 1, PAIRS - 1, PAIRS - 2)

            last_step = STEPS - 1

            def turn_w(n):
                if n == 0:
                    pe.wait_ge(t_done, STEPS // 2)
                    pe.wait_ge(qv_done, STEPS)
                if n == 1:
                    pe.wait_ge(kn_done, STEPS)
                if n == 2:
                    pe.wait_ge(t_done, STEPS)
                if n >= 2:
                    pe.wait_ge(s_tl, TURNS_C + B + n - 1)
                dst = wt_banks[n][:, :].bitcast(bf16)
                for t in range(8):
                    if n < 2:
                        src = w1b[:, t, n * P:(n + 1) * P]
                    else:
                        j, c = 4 * (n - 2) + t // 2, t % 2
                        src = w2b[:, c, j * P:(j + 1) * P]
                    last = pe.transpose(dst[:, t * P:(t + 1) * P], src, identb[:, :])
                last.then_inc(s_wt, 1)

            def turn_x2(b):
                pe.wait_ge(s_xn, B + b + 1)
                if b < 2:
                    pe.wait_ge(exp_done[b], STEPS)
                else:
                    pe.wait_ge(ptl_done[b - 2], STEPS)
                turn_x(x2_banks[b], b)

            def up(m):
                g, j = divmod(m, HT)
                if m < 2:
                    pe.wait_ge(s_wtc[0], 1)
                    pe.wait_ge(s_wtc[1], 1)
                if j == 0:
                    pe.wait_ge(s_tl, TURNS_C + B + 2 * (g + 1))
                if m == 2:
                    pe.wait_ge(ol_done, 2 * STEPS)
                if m >= 3:
                    pe.wait_ge(hr_done, m - 2)
                dst = h_banks[m % 3][:, :].rearrange("p (r t) -> p r t", r=2)
                for c in range(KC):
                    w = w1T[:, c, j * P:(j + 1) * P]
                    pe.matmul(dst, w, xTh[:, 2 * g:2 * g + 2, c, :], start=c == 0, stop=False)
                    last = pe.matmul(dst, w, xTl[:, 2 * g:2 * g + 2, c, :], start=False, stop=c == KC - 1)
                last.then_inc(f1_done, 1)

            turn_w(0)
            turn_w(1)
            project(last_step - 1, 1, PAIRS - 2)
            turn_p(last_step, 0)
            turn_p(last_step, 1)
            turn_x2(0)
            turn_x2(1)
            attend(last_step, 0, B - 1)
            turn_w(2)
            turn_w(3)
            up(0)
            project(last_step, 0, PAIRS - 1)
            attend(last_step, 1, B - 1)
            up(1)
            project(last_step, 1, PAIRS - 1)
            up(2)

            def down(m):
                g, j = divmod(m, HT)
                pe.wait_ge(sl_done, m + 1)
                if m == 0:
                    for q in s_wtc:
                        pe.wait_ge(q, 2)
                if m == HT:
                    pe.wait_ge(x1_done, B)
                    pe.wait_ge(s_tl, TURNS_C + 2 * B)
                for t in range(T4):
                    dst = f_banks[g][t // 2][:, (t % 2) * DIM:(t % 2 + 1) * DIM]
                    s = slice(t * P, (t + 1) * P)
                    for part in (sTh, sTl):
                        last = pe.matmul(dst, part[:, j, s], w2T[:, j, :], start=j == 0 and t % 2 == 0 and part is sTh,
                                         stop=False, skip_group_check=True)
                last.then_inc(f2_done, 1)

            def sums_f(g):
                parts = [ha[:, g, :]]
                if g == 0:
                    pe.wait_ge(ha_done, HT)
                else:
                    pe.wait_ge(ha_done, 2 * HT - 1)
                    pe.wait_ge(h4_done, 2 * HT)
                    parts.append(h4[(2 * HT - 1) % 3])
                for t in range(T4):
                    col = g * T4 + t
                    for n, part in enumerate(parts):
                        last = pe.matmul(fs_bank[:, col:col + 1], part[:, t * P:(t + 1) * P], ones[:, :],
                                         start=n == 0, stop=n == len(parts) - 1)
                last.then_inc(fs_done, 1)

            for m in range(2 * HT):
                if m + 3 < 2 * HT:
                    up(m + 3)
                if m == 2 * HT - 1:
                    sums_f(1)
                down(m)
                if m == 1:
                    turn_x2(2)
                    turn_x2(3)
                if m == HT + 1:
                    sums_f(0)

        @block.vector
        def _(dve):
            def ln_first(b, rows=1):
                ts = range(b * QT, (b + rows) * QT)
                for t in ts:
                    last = dve.bn_stats(stats[:, t, :], xt[:, t, :])
                last.then_inc(s_st, 1)

            def ln_second(b, call, rows=1):
                dve.wait_ge(s_st, call)
                ts = range(b * QT, (b + rows) * QT)
                for t in ts:
                    last = dve.bn_aggr(mv[:, t, :], stats[:, t, :])
                last.then_inc(s_mv, 1)
                dve.wait_ge(s_mv, call)
                s = slice(b * QT, (b + rows) * QT)
                dve.tensor_scalar(lnv[:, s], mv[:, s, 1], EPS, None, ALU.add).then_inc(s_lnv, 1)

            def ln_stats(b, call, rows=1):
                ln_first(b, rows)
                ln_second(b, call, rows)

            def ln_norm(b, call, rows=1):
                dve.wait_ge(s_rstd, call)
                for t in range(b * QT, (b + rows) * QT):
                    last = dve.tensor_scalar(xn[:, t, :], xt[:, t, :], mv[:, t, 0:1], rstd[:, t:t + 1],
                                             ALU.subtract, ALU.mult)
                    if t % QT == QT - 1:
                        last.then_inc(s_xn, 1)

            def low(dst, src, hi):
                return dve.tensor_tensor(dst, src, hi.bitcast(f32), ALU.subtract)

            def turned(n):
                dve.wait_ge(s_th, n + 1)
                if n < TURNS_C:
                    s = slice(4 * n, 4 * n + 4)
                    low(cTl[:, s, :].rearrange(flat3), turn_banks[n][:, :], cTh[:, s, :].rearrange(flat3)).then_inc(s_tl, 1)
                else:
                    b = n - TURNS_C
                    low(xTl[:, b, :, :].rearrange(flat3), turn_banks[n][:, :],
                        xTh[:, b, :, :].rearrange(flat3)).then_inc(s_tl, 1)

            def var_k(n):
                dve.wait_ge(ksq_done, n + 1)
                dve.tensor_reduce(ssk[:, :], ksq[:, :, :], AX.X, ALU.add).then_inc(red_done, 1)

            def norm_k(n):
                dve.wait_ge(rk_done, n + 1)
                dve.tensor_tensor(kn[:, :, :], bB[:, :].rearrange("p (t d) -> p t d", t=UT),
                                  rk[:, :].unsqueeze(2).broadcast_to([P, UT, D]), ALU.mult).then_inc(kn_done, 1)

            def q_lo(n):
                dve.wait_ge(qh_done, n + 1)
                low(ql[:, :, :].rearrange(flat3), bA[:, :], qh[:, :, :].rearrange(flat3)).then_inc(ql_done, 1)

            def pt_lo(i, u):
                dve.wait_ge(pth_done[u], i + 1)
                low(PTl[u][:, :, :].rearrange(flat3), bT[u][:, :], PTh[u][:, :, :].rearrange(flat3)).then_inc(ptl_done[u], 1)

            def k_lo(n):
                dve.wait_ge(kh_done, n + 1)
                dve.scalar_tensor_tensor(kl[:, :, :].rearrange(flat3), bT[1][:, :], gg[:, 0:1],
                                         kh[:, :, :].rearrange(flat3).bitcast(f32),
                                         ALU.mult, ALU.subtract).then_inc(kl_done, 1)

            def o_lo(i, u):
                dve.wait_ge(oh_done, 2 * i + u + 1)
                low(Ol[u][:, :], bO[:, u * SQ:(u + 1) * SQ], Oh[u][:, :]).then_inc(ol_done, 1)

            def var_q(n):
                dve.wait_ge(ssq_done, n + 1)
                dve.tensor_scalar(qv[:, :], bA[:, 0:UT], EPS * D, None, ALU.add).then_inc(qv_done, 1)

            def maxes(n, u):
                dve.wait_ge(s_done[u], n + 1)
                dve.tensor_reduce(mx[u][:, :], bS[u][:, :].rearrange("p (t k) -> p t k", t=QT), AX.X,
                                  ALU.max).then_inc(mx_done[u], 1)
                dve.wait_ge(mx_done[u], n + 1)
                dve.wait_ge(fq_done, n + 1)
                dve.scalar_tensor_tensor(nb[u][:, :], mx[u][:, :], -1.0, fq[:, QT * u:QT * (u + 1)],
                                         ALU.mult, ALU.mult).then_inc(nb_done[u], 1)

            def recip(n, u):
                dve.wait_ge(exp_done[u], n + 1)
                dve.reciprocal(rs[u][:, :], su[u][:, :]).then_inc(rec_done[u], 1)

            def scale_t(i):
                dve.wait_ge(t_sum, i + 1)
                if not known(i) or i >= 1:
                    dve.wait_ge(t_done, i)
                dve.tensor_scalar(gsr[:, :], gsum[:, bass.ds(SG * i, SG)], 0.5 / GROUP, CLIP,
                                  ALU.mult, ALU.max).then_inc(t_scr, 1)

            def compare_t(i):
                dve.wait_ge(t_scr, i + 1)
                w2x = wb[:, bass.ds(SG * i, SG), :]
                scale = gsr[:, :].unsqueeze(2).broadcast_to([P, SG, GROUP])
                dve.tensor_tensor(wpos[:, :, :], w2x, scale, ALU.is_gt)
                dve.scalar_tensor_tensor(wneg[:, :, :], w2x, -1.0, scale, ALU.mult, ALU.is_gt).then_inc(t_pn, 1)

            def residual(b):
                dve.wait_ge(y_done, 2 * PAIRS * (b + 1))
                dst = xt[:, QT * b:QT * (b + 1), :].rearrange(flat3)
                dve.tensor_tensor(dst, bY[:, :], dst, ALU.add).then_inc(x1_done, 1)
                dve.wait_ge(x1_done, b + 1)

            dve.wait_ge(s_x[0], 16)
            ln_stats(0, 1)
            ln_norm(0, 1)
            dve.wait_ge(s_g, 32)
            dve.tensor_tensor(gg[:, :], gqt[:, :], gkt[:, :], ALU.mult).then_inc(s_gg, 1)
            for n in range(TURNS_C + 1):
                turned(n)
            dve.wait_ge(s_x[1], 16)
            ln_stats(1, 2, B - 1)
            var_k(0)
            q_lo(0)
            norm_k(0)
            ln_norm(1, 2, B - 1)

            def ww_lo(n):
                dve.wait_ge(s_wwh, n + 1)
                s = slice(2 * n, 2 * n + 2)
                low(WWl[:, s, :].rearrange(flat3), ww_banks[n % 4][:, :], WWh[:, s, :].rearrange(flat3)).then_inc(s_wwl, 1)

            ww_lo(0)
            k_lo(0)
            ww_lo(1)
            var_q(0)
            for b in range(1, B):
                turned(TURNS_C + b)
            ww_lo(2)
            var_k(1)
            ww_lo(3)
            maxes(0, 0)
            maxes(0, 1)
            ww_lo(4)
            recip(0, 0)
            ww_lo(5)
            ww_lo(6)
            norm_k(1)
            ww_lo(7)
            recip(0, 1)

            def body(i, left=None, stage=None):
                ahead = not known(i) or i + 1 < STEPS
                further = not known(i) or i + 2 < STEPS
                if ahead:
                    q_lo(i + 1)
                if stage == 0:
                    residual(left)
                if ahead:
                    k_lo(i + 1)
                pt_lo(i, 0)
                if ahead:
                    var_q(i + 1)
                if further:
                    var_k(i + 2)
                if ahead:
                    maxes(i + 1, 0)
                o_lo(i, 0)
                pt_lo(i, 1)
                if ahead:
                    maxes(i + 1, 1)
                scale_t(i)
                if ahead:
                    recip(i + 1, 0)
                compare_t(i)
                o_lo(i, 1)
                if further:
                    norm_k(i + 2)
                if stage == 1:
                    ln_first(left)
                if stage == 2:
                    ln_second(left, left + 3)
                if stage == 3:
                    ln_norm(left, left + 3)
                if ahead:
                    recip(i + 1, 1)

            body(0)
            for b in range(B):
                f = b * PAIRS
                if b:
                    for n, stage in enumerate((0, 1, 2, 3)):
                        body(f + n, b - 1, stage)
                with dve.Fori(f + 4 if b else 1, f + PAIRS if b < B - 1 else STEPS - 2) as i:
                    body(i)
            body(STEPS - 2)

            def weights(n):
                dve.wait_ge(s_wt, n + 1)
                dve.tensor_copy((w1T[:, n, :] if n < 2 else w2T[:, 4 * (n - 2):4 * (n - 2) + 4, :].rearrange(flat3)),
                                wt_banks[n][:, :].bitcast(bf16)).then_inc(s_wtc[1], 1)

            def turned_2(b):
                dve.wait_ge(s_th, TURNS_C + B + b + 1)
                low(xTl[:, b, :, :].rearrange(flat3), x2_banks[b][:, :], xTh[:, b, :, :].rearrange(flat3)).then_inc(s_tl, 1)

            def square(m):
                dve.wait_ge(hr_done, m + 1)
                if m >= 3:
                    dve.wait_ge(h4_done, m - 2)
                    dve.wait_ge(sl_done, m - 2)
                dve.tensor_tensor(hs[m % 3], hr[m % 2], hr[m % 2], ALU.mult).then_inc(hs_done, 1)

            def square_lo(m):
                dve.wait_ge(sh_done, m + 1)
                low(sTl[:, m % HT, :], hs[m % 3], sTh[:, m % HT, :]).then_inc(sl_done, 1)

            def mean_square(g):
                dve.wait_ge(fs_done, g + 1)
                dve.tensor_scalar(fv[:, g * T4:(g + 1) * T4], fs_bank[:, g * T4:(g + 1) * T4], 1.0 / HID, EPS_F,
                                  ALU.mult, ALU.add).then_inc(fv_done, 1)

            def finish(g, half):
                dve.wait_ge(fr_done, g + 1)
                dve.wait_ge(f2_done, HT * (g + 1))
                for t in range(2):
                    src = f_banks[g][half][:, t * DIM:(t + 1) * DIM]
                    n = g * T4 + 2 * half + t
                    last = dve.scalar_tensor_tensor(yo[:, n, :], src, fr[:, n:n + 1], xt[:, n, :], ALU.mult, ALU.add)
                last.then_inc(yo_done, 1)

            last_step = STEPS - 1
            scale_t(last_step)
            compare_t(last_step)
            weights(1)
            pt_lo(last_step, 0)
            pt_lo(last_step, 1)
            turned_2(0)
            turned_2(1)
            o_lo(last_step, 0)
            weights(3)
            square(0)
            o_lo(last_step, 1)
            square(1)
            square_lo(0)
            residual(B - 1)
            ln_stats(B - 1, B + 2)
            square(2)
            square_lo(1)
            ln_norm(B - 1, B + 2)
            for m in range(2, 2 * HT):
                if m + 1 < 2 * HT:
                    square(m + 1)
                square_lo(m)
                if m == 4:
                    turned_2(2)
                    turned_2(3)
                if m == HT + 2:
                    mean_square(0)
                if m == HT + 5:
                    finish(0, 0)
                if m == HT + 6:
                    finish(0, 1)
            mean_square(1)
            finish(1, 0)
            finish(1, 1)


_INS = ['x', 'ctx_1024', 'L0_xattn_Wq', 'L0_xattn_Wk', 'L0_xattn_Wv', 'L0_xattn_Wo', 'L0_xattn_gq', 'L0_xattn_gk',
        'L0_ffn_W_fc', 'L0_ffn_W_proj']


def kernel(**inputs):
    import numpy as np
    import concourse.bacc as bacc
    from concourse import mybir
    from concourse.bass_utils import run_bass_kernel_spmd

    nc = bacc.Bacc("TRN2", target_bir_lowering=False, num_devices=1)
    arrays, args = {}, []
    for name in _INS:
        a = np.ascontiguousarray(inputs[name])
        arrays[f"in_{name}"] = a
        args.append(nc.dram_tensor(f"in_{name}", a.shape, mybir.dt.from_np(a.dtype), kind="ExternalInput").ap())
    args.append(nc.dram_tensor("out", arrays["in_x"].shape, mybir.dt.float32, kind="ExternalOutput").ap())
    xattn_ffn(nc, *args)
    r = run_bass_kernel_spmd(nc, [arrays], core_ids=[0])
    return r.results[0]["out"]
```
